# Optimizing a Trainium2 kernel written in Bass

```python
import numpy as np
import jax
import jax.numpy as jnp

def _softmax(x, axis=-1):
    return jax.nn.softmax(x, axis=axis)

def _gelu(x):
    return jax.nn.gelu(x, approximate=True)

def _silu(x):
    return jax.nn.silu(x)

def _sigmoid(x):
    return jax.nn.sigmoid(x)

def _layernorm(x, axis=-1, eps=1e-05):
    m = jnp.mean(x, axis=axis, keepdims=True)
    v = jnp.var(x, axis=axis, keepdims=True)
    return (x - m) / jnp.sqrt(v + eps)

def _scatter_add(tgt, idx, src, axis=0):
    return tgt.at[idx].add(src)

def _segment_sum(src, seg, n):
    return jax.ops.segment_sum(src, seg, n)
kernel_name = 'mk_conv_preact_d2_conv_nchw32_r2_8fecf5'

def setup_inputs(seed: int=0):
    np.random.seed(seed)
    _w = jnp.asarray

    def _rec_inputs():
        import jax
        import jax.numpy as jnp
        _gk = jax.random.key(seed)
        x = -9.26e-05 + 0.9999 * jax.random.normal(jax.random.fold_in(_gk, 1), (8, 32, 192, 192), jnp.float32)
        return x
    x = _rec_inputs()

    def _L0_conv_setup():
        import jax, jax.numpy as jnp
        import numpy as np
        B, C, H, W = (8, 32, 192, 192)
        PLANES, K, P, D, OFFSET = (32, 3, 1, 1, 1)

        def conv2d(x, w, b, pad, dil=1):
            out = jax.lax.conv_general_dilated(x, w, window_strides=(1, 1), padding=[(pad, pad), (pad, pad)], rhs_dilation=(dil, dil), dimension_numbers=('NCHW', 'OIHW', 'NCHW'))
            return out + b[None, :, None, None]

        def reflect(t, rng):
            two = 2.0 * rng
            m = jnp.mod(jnp.abs(t), two)
            r = jnp.where(m > rng, two - m, m)
            return jnp.clip(r, 0.0, rng)
        key = jax.random.key(seed)
        k1, k2, k3 = jax.random.split(key, 3)
        x = jax.random.normal(k1, (B, C, H, W), dtype=jnp.float32)
        koff = 2 * OFFSET + 1
        w_off = jax.random.normal(k2, (2 * C, C, koff, koff), dtype=jnp.float32) * (1.0 / np.sqrt(C * koff * koff))
        b_off = jnp.zeros((2 * C,), dtype=jnp.float32)
        w_dcn = jax.random.normal(k3, (PLANES, C, K, K), dtype=jnp.float32) * (1.0 / np.sqrt(C * K * K))
        b_dcn = jnp.zeros((PLANES,), dtype=jnp.float32)
        return {'x': x, 'w_off': w_off, 'b_off': b_off, 'w_dcn': w_dcn, 'b_dcn': b_dcn}
    _L0_conv_all = _L0_conv_setup()
    _L0_conv_in = {k: v for k, v in _L0_conv_all.items() if k in ('w_off', 'b_off', 'w_dcn', 'b_dcn')}
    del _L0_conv_all

    def _L1_conv_setup():
        import jax, jax.numpy as jnp
        import numpy as np
        from jax import lax
        B, C, H, W = (16, 32, 192, 192)
        NK = 32
        K = 3
        HID = 64
        key = jax.random.key(seed)
        ks = jax.random.split(key, 5)
        x = jax.random.normal(ks[0], (B, C, H, W), dtype=jnp.float32)
        w1 = jax.random.normal(ks[1], (C, HID), dtype=jnp.float32) * (1.0 / np.sqrt(C))
        b1 = jnp.zeros((HID,), dtype=jnp.float32)
        w2 = jax.random.normal(ks[2], (HID, NK * K * K), dtype=jnp.float32) * (1.0 / np.sqrt(HID))
        b2 = jnp.zeros((NK * K * K,), dtype=jnp.float32)
        return {'x': x, 'w1': w1, 'b1': b1, 'w2': w2, 'b2': b2}
    _L1_conv_all = _L1_conv_setup()
    _L1_conv_in = {k: v for k, v in _L1_conv_all.items() if k in ('w1', 'b1', 'w2', 'b2')}
    del _L1_conv_all
    return {'x': x, 'L0_conv_w_off': _L0_conv_in['w_off'], 'L0_conv_b_off': _L0_conv_in['b_off'], 'L0_conv_w_dcn': _L0_conv_in['w_dcn'], 'L0_conv_b_dcn': _L0_conv_in['b_dcn'], 'L1_conv_w1': _L1_conv_in['w1'], 'L1_conv_b1': _L1_conv_in['b1'], 'L1_conv_w2': _L1_conv_in['w2'], 'L1_conv_b2': _L1_conv_in['b2']}

def reference(x, L0_conv_w_off, L0_conv_b_off, L0_conv_w_dcn, L0_conv_b_dcn, L1_conv_w1, L1_conv_b1, L1_conv_w2, L1_conv_b2):
    import jax
    import jax.numpy as jnp

    def _L0_conv_ref(x, w_off, b_off, w_dcn, b_dcn):
        import jax, jax.numpy as jnp
        import numpy as np
        B, C, H, W = (8, 32, 192, 192)
        PLANES, K, P, D, OFFSET = (32, 3, 1, 1, 1)

        def conv2d(x, w, b, pad, dil=1):
            out = jax.lax.conv_general_dilated(x, w, window_strides=(1, 1), padding=[(pad, pad), (pad, pad)], rhs_dilation=(dil, dil), dimension_numbers=('NCHW', 'OIHW', 'NCHW'))
            return out + b[None, :, None, None]

        def reflect(t, rng):
            two = 2.0 * rng
            m = jnp.mod(jnp.abs(t), two)
            r = jnp.where(m > rng, two - m, m)
            return jnp.clip(r, 0.0, rng)
        b, c, h, w = x.shape
        n = b * c
        off = (jax.nn.sigmoid(conv2d(x, w_off, b_off, OFFSET * D, D)) - 0.5) * (2.0 * OFFSET)
        off = off.reshape(n, 2, h, w)
        offx = off[:, 0] / (w - 1)
        offy = off[:, 1] / (h - 1)
        gy_base = jnp.arange(h, dtype=jnp.float32) / (h - 1) * 2.0 - 1.0
        gx_base = jnp.arange(w, dtype=jnp.float32) / (w - 1) * 2.0 - 1.0
        gx = gx_base[None, None, :] - offx
        gy = gy_base[None, :, None] - offy
        ix = reflect((gx + 1.0) * 0.5 * (w - 1), float(w - 1))
        iy = reflect((gy + 1.0) * 0.5 * (h - 1), float(h - 1))
        ix0 = jnp.floor(ix)
        iy0 = jnp.floor(iy)
        wx = ix - ix0
        wy = iy - iy0
        i0 = jnp.clip(ix0, 0, w - 1).astype(jnp.int32)
        i1 = jnp.clip(ix0 + 1, 0, w - 1).astype(jnp.int32)
        j0 = jnp.clip(iy0, 0, h - 1).astype(jnp.int32)
        j1 = jnp.clip(iy0 + 1, 0, h - 1).astype(jnp.int32)
        planes = x.reshape(n, h, w)
        nidx = jnp.arange(n)[:, None, None]
        v00 = planes[nidx, j0, i0]
        v01 = planes[nidx, j0, i1]
        v10 = planes[nidx, j1, i0]
        v11 = planes[nidx, j1, i1]
        sampled = v00 * (1 - wy) * (1 - wx) + v01 * (1 - wy) * wx + v10 * wy * (1 - wx) + v11 * wy * wx
        out = sampled.reshape(b, c, h, w)
        return conv2d(out, w_dcn, b_dcn, P, D)

    def _L1_conv_ref(x, w1, b1, w2, b2):
        import jax, jax.numpy as jnp
        import numpy as np
        from jax import lax
        B, C, H, W = (16, 32, 192, 192)
        NK = 32
        K = 3
        HID = 64
        b, c, h, w = x.shape
        pooled = x.mean(axis=(2, 3))
        hdn = jax.nn.relu(pooled @ w1 + b1)
        kernels = (hdn @ w2 + b2).reshape(b, NK, K, K)
        xg = x[:, :NK].reshape(1, b * NK, h, w)
        wgt = kernels.reshape(b * NK, 1, K, K)
        pad = K // 2
        out = lax.conv_general_dilated(xg, wgt, window_strides=(1, 1), padding=[(pad, pad), (pad, pad)], feature_group_count=b * NK, dimension_numbers=('NCHW', 'OIHW', 'NCHW'))
        return out.reshape(b, NK, h, w)

    def _gn(v, G=16, eps=1e-05):
        B_, C_, H_, W_ = v.shape
        g = v.reshape(B_, G, C_ // G, H_, W_)
        m = jnp.mean(g, axis=(2, 3, 4), keepdims=True)
        s = jnp.var(g, axis=(2, 3, 4), keepdims=True)
        return ((g - m) / jnp.sqrt(s + eps)).reshape(v.shape)

    def _ln_c(v, eps=1e-06):
        m = jnp.mean(v, axis=1, keepdims=True)
        s = jnp.var(v, axis=1, keepdims=True)
        return (v - m) / jnp.sqrt(s + eps)

    def _ln_t(v, eps=1e-05):
        m = jnp.mean(v, axis=-1, keepdims=True)
        s = jnp.var(v, axis=-1, keepdims=True)
        return (v - m) / jnp.sqrt(s + eps)

    def _to_tokens(v):
        B_, C_, H_, W_ = v.shape
        return v.reshape(B_, C_, H_ * W_).transpose(0, 2, 1)

    def _from_tokens(t, like):
        B_, C_, H_, W_ = like.shape
        return t.transpose(0, 2, 1).reshape(B_, C_, H_, W_)
    x = x + _L0_conv_ref(_gn(x), L0_conv_w_off, L0_conv_b_off, L0_conv_w_dcn, L0_conv_b_dcn)
    x = x + _L1_conv_ref(_gn(x), L1_conv_w1, L1_conv_b1, L1_conv_w2, L1_conv_b2)
    return x

_drawn_inputs = setup_inputs


def setup_inputs(seed=0):
    import zlib

    import numpy as np

    out = dict(_drawn_inputs(seed))
    spreads = {'L0_conv_b_off': (0.0, 0.268),
     'L0_conv_b_dcn': (0.0, 0.1),
     'L1_conv_b1': (0.0, 0.1),
     'L1_conv_b2': (0.0, 0.1)}
    factors = {}
    for name, (base, spread) in spreads.items():
        noise = np.random.default_rng([zlib.crc32(name.encode()), seed]).standard_normal(out[name].shape)
        drawn = base * np.exp(spread * noise) if base else spread * noise
        out[name] = jnp.asarray(drawn.astype(out[name].dtype))
    for name, factor in factors.items():
        out[name] = (out[name] * factor).astype(out[name].dtype)
    return out
```

```python
from contextlib import ExitStack

import numpy as np

import concourse.bass as bass
from concourse import mybir

F32 = mybir.dt.float32
BF16 = mybir.dt.bfloat16
U16 = mybir.dt.uint16
ALU = mybir.AluOpType
ACT = mybir.ActivationFunctionType
AX = mybir.AxisListType

P = 128
C = 32
G = P // C
B, H, W = 8, 192, 192
HW = H * W
WP = W + 2
NB = 4
CHUNKS = H // (G * NB)
HALF = NB // 2
N = NB * W
NH = HALF * W
BLOCKS = H // G
HID = 64
EPS = 1e-5
CNT = HW // G
STILES = 8
SBLOCKS = BLOCKS // STILES
SW = SBLOCKS * W
XS, SS, CS = 3, 3, 4
ABOVE, MID, BELOW = 0, 1, 2
BANK = 512
K_AVG, K_EYE, K_CEN = slice(0, P), slice(P, P + C), slice(P + C, P + C + 6)
M_REL, M_SQ, M_LOC, V_SQ, V_LOC, DEV, DEV_SQ, V_ALL, V_EPS, D_STD = (
    slice(i, i + 1) for i in range(10))
C_XM, C_XV, C_OB, C_DB, C_YM, C_YV, C_HID, C_TAP, C_WB = 0, 1, 2, 4, 5, 6, 7, 8, 14
BANDS = [(g, o) for o in range(2) for g in range(G) if 0 <= g - o <= 2]
LOADED = 16 * (1 + 5 * len(BANDS) + 3 * G + 1)
X_STEPS, Y_STEPS = 9, 14
LERPS = 6
PADDED = 4


def x_dmas(j):
    return 3 + (j in (0, CHUNKS - 1))


def s_dmas(j):
    return 4 + (j % SS == SS - 1 and j != CHUNKS - 1) + (j % SS == 0 and j != 0)


def ring_total(b, j, slots, dmas):
    mine = range(j % slots, CHUNKS, slots)
    return b * (16 * sum(dmas(i) for i in mine)) + 16 * sum(dmas(i) for i in mine if i <= j)


def ring_before(b, j, slots, dmas):
    return ring_total(b, j, slots, dmas) - 16 * dmas(j)


def wait(eng, sem, value):
    if not isinstance(value, int) or value > 0:
        eng.wait_ge(sem, value)


def pads_set(b, j):
    return PADDED * b + (min(j, 2) + 1 if j < CHUNKS - 1 else PADDED)


def small_base(b):
    if isinstance(b, int):
        if b == 0:
            return 3
        if b == B:
            return 7 + 9 * (B - 2) + 6
    return (b - 1) * 9 + 7


def block_kernel(nc, x, w_off, b_off, w_dcn, b_dcn, w1, b1, w2, b2, consts, out):
    with ExitStack() as ctx:
        def sb(name, shape, dt=F32):
            return ctx.enter_context(nc.sbuf_tensor(name, shape, dt))

        def sem(name):
            return ctx.enter_context(nc.semaphore(name))

        xv = [sb(f"xv{s}", [P, 3, NB, WP]) for s in range(XS)]
        nb = [sb(f"nb{s}", [P, 3, NB, W]) for s in range(2)]
        du = [sb(f"du{s}", [P, NB, W]) for s in range(2)]
        dv = [sb(f"dv{s}", [P, NB, W]) for s in range(2)]
        mu = [sb(f"mu{s}", [P, NB, W], BF16) for s in range(2)]
        mv = [sb(f"mv{s}", [P, NB, W], BF16) for s in range(2)]
        sc = [sb(f"sc{s}", [P, NB, WP]) for s in range(2)]
        sa = sb("sa", [P, SS * NB, WP])
        sw = sb("sw", [P, SS * NB, WP])
        yc = [sb(f"yc{s}", [P, NB, W]) for s in range(CS)]
        ya = sb("ya", [P, BLOCKS, WP])
        yb = sb("yb", [P, BLOCKS, WP])
        ot = [sb(f"ot{s}", [P, NB, W]) for s in range(2)]
        st = [sb(f"st{s}", [P, SW]) for s in range(2)]
        junk = sb("junk", [P, N], BF16)
        wo = sb("wo", [P, 2, 3, 2 * C])
        wos = sb("wos", [P, 2, 3, 2 * C])
        wd = sb("wd", [P, 3, 2 * C])
        wds = sb("wds", [P, 3, 2 * C])
        wy = sb("wy", [P, 3, 2 * C])
        w1r = sb("w1r", [P, HID])
        w2r = sb("w2r", [HID, 6, P])
        b2r = sb("b2r", [P, 6])
        b1c = sb("b1c", [HID, 1])
        bo = sb("bo", [P, 2])
        bd = sb("bd", [P, 1])
        kc = sb("kc", [P, P + C + 6])
        zero = sb("zero", [P, 2 * WP])
        xs1 = sb("xs1", [P, STILES])
        xs2 = sb("xs2", [P, STILES])
        ys1 = sb("ys1", [P, 2 * CHUNKS])
        ys2 = sb("ys2", [P, CHUNKS])
        xn = sb("xn", [P, 16])
        yn = sb("yn", [P, 16])
        half = sb("half", [P, 1])
        npiv = sb("npiv", [P, 1])
        mx = sb("mx", [P, 1])
        vx = sb("vx", [P, 1])
        rx = sb("rx", [P, 1])
        nmx = sb("nmx", [P, 1])
        mxs = sb("mxs", [P, 1])
        mxp = sb("mxp", [P, 1])
        nmy = sb("nmy", [P, 1])
        my = sb("my", [P, 1])
        vy = sb("vy", [P, 1])
        ry = sb("ry", [P, 1])
        my_neg = sb("my_neg", [P, 1])
        pooled = sb("pooled", [P, 1])
        hid = sb("hid", [HID, 1])
        tapr = sb("tapr", [P, 6])
        tap = sb("tap", [P, 6])
        ob = sb("ob", [P, 2])
        db = sb("db", [P, 1])
        wb = sb("wb", [P, 1])

        z = ctx.enter_context(nc.psum_tensor("z", [P, 2, 2, BANK], F32))
        dc = ctx.enter_context(nc.psum_tensor("dc", [P, 2, BANK], F32))
        dw = ctx.enter_context(nc.psum_tensor("dw", [P, BANK], F32))
        sm = ctx.enter_context(nc.psum_tensor("sm", [P, BANK], F32))

        loaded = sem("loaded")
        cleared = sem("cleared")
        x_in = [sem(f"x_in{s}") for s in range(XS)]
        st_in = [sem(f"st_in{s}") for s in range(2)]
        y_in = [sem(f"y_in{s}") for s in range(CS)]
        s_sh = [sem(f"s_sh{s}") for s in range(SS)]
        y_sh = [sem(f"y_sh{s}") for s in range(CS)]
        o_out = [sem(f"o_out{s}") for s in range(2)]
        piv = sem("piv")
        centred = sem("centred")
        bo_half = sem("bo_half")
        st_used = sem("st_used")
        x_row = sem("x_row")
        y_row = sem("y_row")
        pads = sem("pads")
        off_mm = sem("off_mm")
        z_read = sem("z_read")
        mirror = sem("mirror")
        sided = sem("sided")
        prepped = sem("prepped")
        lerp = sem("lerp")
        x_free = sem("x_free")
        sampled = sem("sampled")
        dcn_mm = sem("dcn_mm")
        y_done = sem("y_done")
        y_sq = sem("y_sq")
        dw_mm = sem("dw_mm")
        o_done = sem("o_done")
        small = sem("small")
        small_rd = sem("small_rd")
        x_tot = sem("x_tot")
        y_tot = sem("y_tot")
        x_step = sem("x_step")
        y_step = sem("y_step")
        wo_ok = sem("wo_ok")
        wd_ok = sem("wd_ok")
        wy_ok = sem("wy_ok")
        mxs_ok = sem("mxs_ok")
        mxp_ok = sem("mxp_ok")
        nmy_ok = sem("nmy_ok")
        passed = sem("passed")
        block = ctx.enter_context(nc.Block())

        lines = x.rearrange("b h c w -> b (h c) w")
        lines_out = out.rearrange("b h c w -> b (h c) w")

        def blocks_of(t, b, first, count):
            return t[b, first:first + P * count, :].rearrange("(k p) w -> p k w", p=P)

        def wait_apart(eng, sem, value):
            if not isinstance(value, int):
                eng.wait_ge(sem, value)
                eng.sem_inc(passed, 1)
            elif value > 0:
                eng.wait_ge(sem, value)

        def cid(b, j):
            return b * CHUNKS + j

        def all_steps(eng, step):
            def image(b, last, own, nxt, prev, prev2):
                for j in range(last):
                    step(b, j, own, nxt, prev, prev2)
            image(0, CHUNKS, True, True, False, False)
            image(1, CHUNKS, True, True, True, False)
            with eng.Fori(2, B - 1) as b:
                image(b, CHUNKS, True, True, True, True)
            image(B - 1, CHUNKS, True, False, True, True)
            image(B, CHUNKS, False, False, True, True)
            image(B + 1, 2, False, False, False, True)

        def dw_at(b, j, prev, prev2):
            if j >= 2:
                return (b - 1, j - 2) if prev else None
            return (b - 2, CHUNKS - 2 + j) if prev2 else None

        def dcn_at(b, j, own, prev):
            if j >= 2:
                return [(b, j - 2)] if own else []
            if j == 0 and prev:
                return [(b - 1, CHUNKS - 2), (b - 1, CHUNKS - 1)]
            return []

        def y_at(b, j, own, prev):
            if j >= 3:
                return [(b, j - 3)] if own else []
            if j == 0 and prev:
                return [(b - 1, CHUNKS - 3)]
            if j == 1 and prev:
                return [(b - 1, CHUNKS - 2), (b - 1, CHUNKS - 1)]
            return []

        @block.sync
        def _(sp):
            def x_load(b, j):
                s, k = j % XS, j * NB
                n = cid(b, j)
                wait_apart(sp, x_free, n - XS + 1)
                pj = j - XS
                pb = b if pj >= 0 else b - 1
                if not (isinstance(pb, int) and pb < 0):
                    wait_apart(sp, y_in[pj % CS], ring_total(pb, pj % CHUNKS, CS, lambda i: 1))
                v, done = xv[s], x_in[s]
                for view in range(3):
                    line, k0, k1 = P * k + C * (view - 1), 0, NB
                    if j == 0 and view == ABOVE:
                        sp.dma_start(v[C:P, view, 0, 1:W + 1], lines[b, 0:P - C, :]).then_inc(done, 16)
                        k0 = 1
                    if j == CHUNKS - 1 and view == BELOW:
                        sp.dma_start(v[0:P - C, view, NB - 1, 1:W + 1], lines[b, H * C - P + C:H * C, :])\
                            .then_inc(done, 16)
                        k1 = NB - 1
                    sp.dma_start(v[:, view, k0:k1, 1:W + 1],
                                 blocks_of(lines, b, line + P * k0, k1 - k0)).then_inc(done, 16)

            def st_load(b, i):
                wait_apart(sp, st_used, b * STILES + i - 1)
                sp.dma_start(st[i % 2][:].rearrange("p (k w) -> p k w", w=W),
                             blocks_of(lines, b, P * SBLOCKS * i, SBLOCKS)).then_inc(st_in[i % 2], 16)

            def residual(b, j):
                s = j % CS
                n = cid(b, j)
                wait_apart(sp, x_in[j % XS], ring_total(b, j, XS, x_dmas))
                wait_apart(sp, y_sh[s], ring_before(b, j, CS, lambda i: 4))
                wait_apart(sp, y_sq, n - CS + 1)
                sp.dma_start(yc[s][:], xv[j % XS][:, MID, :, 1:W + 1]).then_inc(y_in[s], 16)

            def s_shift(b, j):
                n, s, k = cid(b, j), j % SS, (j % SS) * NB
                q, done = sc[j % 2], s_sh[j % SS]
                wait_apart(sp, sampled, n + 1)
                wait_apart(sp, dcn_mm, 2 * (n - 1))
                sp.dma_start(sa[C:P, k:k + NB, :], q[0:P - C, :, :]).then_inc(done, 16)
                sp.dma_start(sw[0:P - C, k:k + NB, :], q[C:P, :, :]).then_inc(done, 16)
                top, bottom = slice(0, C), slice(P - C, P)
                if s == SS - 1:
                    sp.dma_start(sa[top, k + 1:k + NB, :], q[bottom, 0:NB - 1, :]).then_inc(done, 16)
                    if j != CHUNKS - 1:
                        sp.dma_start(sa[top, 0:1, :], q[bottom, NB - 1:NB, :]).then_inc(done, 16)
                else:
                    sp.dma_start(sa[top, k + 1:k + NB + 1, :], q[bottom, :, :]).then_inc(done, 16)
                if s == 0:
                    sp.dma_start(sw[bottom, 0:NB - 1, :], q[top, 1:NB, :]).then_inc(done, 16)
                    if j != 0:
                        sp.dma_start(sw[bottom, SS * NB - 1:SS * NB, :], q[top, 0:1, :]).then_inc(done, 16)
                else:
                    sp.dma_start(sw[bottom, k - 1:k + NB - 1, :], q[top, :, :]).then_inc(done, 16)

            def y_shift(b, j):
                n, k, q, done = cid(b, j), j * NB, yc[j % CS], y_sh[j % CS]
                wait_apart(sp, y_done, 2 * (n + 1))
                nxt = j + 2 if j < CHUNKS - 1 else j + 1
                wait_apart(sp, dw_mm, 2 * (cid(b - 1, nxt)))
                sp.dma_start(ya[C:P, k:k + NB, 1:W + 1], q[0:P - C]).then_inc(done, 16)
                sp.dma_start(yb[0:P - C, k:k + NB, 1:W + 1], q[C:P]).then_inc(done, 16)
                top, bottom = slice(0, C), slice(P - C, P)
                m = NB - (j == CHUNKS - 1)
                sp.dma_start(ya[top, k + 1:k + 1 + m, 1:W + 1], q[bottom, 0:m]).then_inc(done, 16)
                m = int(j == 0)
                sp.dma_start(yb[bottom, k + m - 1:k + NB - 1, 1:W + 1], q[top, m:NB]).then_inc(done, 16)

            def store(b, j):
                n, s = cid(b, j), j % 2
                wait_apart(sp, o_done, 2 * (n + 1))
                sp.dma_start(blocks_of(lines_out, b, P * NB * j, NB), ot[s][:]).then_inc(o_out[s], 16)

            sp.dma_start(kc[:], consts).then_inc(loaded, 16)
            for i in range(2):
                st_load(0, i)
            sp.wait_ge(cleared, 4)
            for g, o in BANDS:
                c, m, t = slice(C * g, C * g + C), slice(C * o, C * o + C), slice(3 * o, 3 * o + 3)
                for i in range(2):
                    sp.dma_start(wo[c, i, :, m], w_off[g - o, i]).then_inc(loaded, 16)
                sp.dma_start(wd[c, :, m], w_dcn[g - o]).then_inc(loaded, 16)
                sp.dma_start(w2r[:, t, c], w2[g - o]).then_inc(loaded, 16)
                sp.dma_start(b2r[c, t], b2[g - o]).then_inc(loaded, 16)
            for g in range(G):
                c = slice(C * g, C * g + C)
                sp.dma_start(bo[c, :], b_off).then_inc(loaded, 16)
                sp.dma_start(bd[c, :], b_dcn).then_inc(loaded, 16)
                sp.dma_start(w1r[c, :], w1).then_inc(loaded, 16)
            sp.dma_start(b1c[:], b1).then_inc(loaded, 16)
            x_load(0, 0)
            for i in range(2, STILES):
                st_load(0, i)

            def step(b, j, own, nxt, prev, prev2):
                if own and j < CHUNKS - 1:
                    x_load(b, j + 1)
                if nxt and j == CHUNKS - 1:
                    x_load(b + 1, 0)
                if nxt and j < STILES:
                    st_load(b + 1, j)
                if own:
                    residual(b, j)
                before = dw_at(b, j - 1, prev, prev2) if j else (
                    (b - 2, CHUNKS - 3) if prev2 else None)
                if before:
                    store(*before)
                if j:
                    if own:
                        s_shift(b, j - 1)
                elif prev:
                    s_shift(b - 1, CHUNKS - 1)
                for y in y_at(b, j, own, prev):
                    y_shift(*y)

            all_steps(sp, step)
            store(B - 1, CHUNKS - 1)
            for s in range(2):
                sp.wait_ge(o_out[s], 16 * B * CHUNKS // 2)

        @block.tensor
        def _(pe):
            halves = (slice(0, 2 * C), slice(2 * C, P))

            def conv(acc, weights, above, below):
                for kx in range(3):
                    for m, view in zip(halves, (above, below)):
                        last = nc.tensor.matmul(acc[m, :], weights[:, kx, :], view[:, :, kx:kx + W],
                                                start=kx == 0, stop=kx == 2)
                return last

            def offsets(b, j, i):
                n, s = cid(b, j), j % XS
                if i == 0:
                    pe.wait_ge(x_in[s], ring_total(b, j, XS, x_dmas))
                    pe.wait_ge(pads, pads_set(b, j))
                    if j == 0:
                        pe.wait_ge(wo_ok, b + 1)
                wait(pe, z_read, 2 * (n - 1) + i + 1)
                for h in range(2):
                    k = slice(HALF * h, HALF * h + HALF)
                    last = conv(z[:, i, h, 0:NH], wos[:, i], xv[s][:, ABOVE, k, :], xv[s][:, BELOW, k, :])
                last.then_inc(off_mm, 1)

            def deform(b, j, h):
                n, k = cid(b, j), (j % SS) * NB + HALF * h
                if h == 0:
                    if j == 0:
                        pe.wait_ge(wd_ok, b + 1)
                    for i in (j - 1, j, j + 1):
                        if 0 <= i < CHUNKS:
                            pe.wait_ge(s_sh[i % SS], ring_total(b, i, SS, s_dmas))
                    pe.wait_ge(sampled, cid(b, min(j + 1, CHUNKS - 1)) + 1)
                wait(pe, y_done, 2 * (n - 1) + h + 1)
                conv(dc[:, h, 0:NH], wds, sa[:, k:k + HALF, :], sw[:, k:k + HALF, :]).then_inc(dcn_mm, 1)

            def depthwise(b, j, h):
                n, k = cid(b, j), j * NB + HALF * h
                if h == 0 and j == 0:
                    pe.wait_ge(wy_ok, b + 1)
                    for i in range(CHUNKS - CS, CHUNKS):
                        pe.wait_ge(y_sh[i % CS], ring_total(b, i, CS, lambda i: 4))
                wait(pe, o_done, 2 * n + h)
                conv(dw[:, 0:NH], wy, ya[:, k:k + HALF, :], yb[:, k:k + HALF, :]).then_inc(dw_mm, 1)

            def average(col, src, count):
                wait(pe, small_rd, count)
                nc.tensor.matmul(sm[:, col:col + 1], kc[:, K_AVG], src, start=True, stop=True)\
                    .then_inc(small, 1)

            def biases(cols, sets, mean, count):
                wait(pe, small_rd, count)
                for col, weights in zip(cols, sets):
                    for kx in range(3):
                        for m in halves:
                            last = nc.tensor.matmul(sm[m, col:col + 1], weights[:, kx, :], mean,
                                                    start=kx == 0, stop=kx == 2)
                last.then_inc(small, 1)

            pe.wait_ge(loaded, LOADED)

            def x_norm_mm(b, i, base):
                pe.wait_ge(x_step, X_STEPS * b + (1, 7)[i])
                average((C_XM, C_XV)[i], (xn[:, M_LOC], xn[:, V_ALL])[i], base + i)

            x_norm_mm(0, 0, 0)
            x_norm_mm(0, 1, 0)
            pe.wait_ge(wo_ok, 1)
            biases((C_OB, C_OB + 1), (wos[:, 0], wos[:, 1]), nmx[:], 2)

            def step(b, j, own, nxt, prev, prev2):
                base = small_base(b)
                k = 4 if prev else 0
                dwc, dcs = dw_at(b, j, prev, prev2), dcn_at(b, j, own, prev)
                if own:
                    offsets(b, j, 0)
                if j == 1 and prev:
                    pe.wait_ge(y_tot, b)
                    average(C_YM, yn[:, M_LOC], base)
                if j == 10 and nxt:
                    x_norm_mm(b + 1, 0, base + k + (2 if prev else 1))
                if own:
                    offsets(b, j, 1)
                if j == 1 and prev:
                    pe.wait_ge(y_step, Y_STEPS * (b - 1) + 7)
                    average(C_YV, yn[:, V_ALL], base + 1)
                if j == 10 and nxt:
                    x_norm_mm(b + 1, 1, base + k + (2 if prev else 1))
                if j == 2 and prev:
                    pe.wait_ge(wy_ok, b)
                    biases((C_WB,), (wy,), my_neg[:], base + 4 + (1 if own else 0))
                for h in range(2):
                    if dwc:
                        depthwise(*dwc, h)
                    if j == 1 and prev and h == 0:
                        pe.wait_ge(y_step, Y_STEPS * (b - 1) + 11)
                        wait(pe, small_rd, base + 2)
                        nc.tensor.matmul(sm[0:HID, C_HID:C_HID + 1], w1r[:], pooled[:],
                                         start=True, stop=True).then_inc(small, 1)
                    for d in dcs[:1]:
                        deform(*d, h)
                for d in dcs[1:]:
                    for h in range(2):
                        deform(*d, h)
                if j == 1 and prev:
                    pe.wait_ge(small_rd, base + 3)
                    for t in range(6):
                        last = nc.tensor.matmul(sm[:, C_TAP + t:C_TAP + t + 1], w2r[:, t, :], hid[:],
                                                start=True, stop=True)
                    last.then_inc(small, 1)
                if j == 1 and own:
                    pe.wait_ge(wd_ok, b + 1)
                    biases((C_DB,), (wds,), nmx[:], base + k)
                if j == CHUNKS - 1 and nxt:
                    pe.wait_ge(wo_ok, b + 2)
                    biases((C_OB, C_OB + 1), (wos[:, 0], wos[:, 1]), nmx[:],
                           base + k + (4 if prev else 3))

            all_steps(pe, step)

        @block.scalar
        def _(act):
            def offsets(b, j, i):
                n, s = cid(b, j), j % 2
                d, m = ((du, mu), (dv, mv))[i]
                act.wait_ge(off_mm, 2 * n + i + 1)
                wait(act, sampled, n - 1)
                nc.scalar.activation(d[s][:].rearrange("p (h k) w -> p h (k w)", h=2),
                                     z[:, i, :, 0:NH], ACT.Tanh, bias=ob[:, i:i + 1], scale=0.5)\
                    .then_inc(z_read, 1)
                act.wait_ge(z_read, 2 * n + i + 1)
                nc.scalar.activation(m[s][:], d[s][:], ACT.Relu, scale=-1.0).then_inc(prepped, 1)
                nc.scalar.activation(d[s][:], d[s][:], ACT.Abs, scale=0.5).then_inc(prepped, 1)

            def sides(b, j):
                n, s, v = cid(b, j), j % 2, xv[j % XS]
                act.wait_ge(x_in[j % XS], ring_total(b, j, XS, x_dmas))
                act.wait_ge(pads, pads_set(b, j))
                wait(act, sampled, n - 1)
                nc.scalar.activation(nb[s][:, :, :, 1:W], v[:, :, :, 1:W], ACT.Copy)
                nc.scalar.activation(nb[s][:, :, :, 0:1], v[:, :, :, 2:3], ACT.Copy).then_inc(sided, 1)

            def mirror_row(b, j):
                s, v = j % 2, xv[j % XS]
                q, k, to, of = ((slice(0, C), 0, ABOVE, BELOW) if j == 0 else
                                (slice(P - C, P), NB - 1, BELOW, ABOVE))
                act.wait_ge(sided, cid(b, j) + 1)
                nc.scalar.activation(v[q, to, k, 1:W + 1], v[q, of, k, 1:W + 1], ACT.Copy)
                nc.scalar.activation(nb[s][q, to, k, :], nb[s][q, of, k, :], ACT.Copy).then_inc(mirror, 1)

            def finish(b, j, h):
                n, s = cid(b, j), j % 2
                act.wait_ge(dw_mm, 2 * n + h + 1)
                if h == 0:
                    pj = j - 2
                    pb = b if pj >= 0 else b - 1
                    if not (isinstance(pb, int) and pb < 0):
                        act.wait_ge(o_out[s], ring_total(pb, pj % CHUNKS, 2, lambda i: 1))
                nc.scalar.activation(ot[s][:, HALF * h:HALF * h + HALF, :].rearrange("p k w -> p (k w)"),
                                     dw[:, 0:NH], ACT.Identity, bias=wb[:]).then_inc(o_done, 1)

            def x_sums(b, i):
                s = i % 2
                act.wait_ge(st_in[s], b * (16 * STILES // 2) + 16 * (i // 2 + 1))
                if i == 0:
                    act.wait_ge(piv, b + 1)
                nc.scalar.activation(st[s][:], st[s][:], ACT.Identity, bias=npiv[:],
                                     accum_out=xs1[:, i:i + 1]).then_inc(centred, 1)
                act.wait_ge(centred, b * STILES + i + 1)
                nc.scalar.activation(st[s][:], st[s][:], ACT.Square,
                                     accum_out=xs2[:, i:i + 1]).then_inc(st_used, 1)

            def y_square(b, j):
                n, s = cid(b, j), j % CS
                act.wait_ge(y_done, 2 * (n + 1))
                if j == 0:
                    act.wait_ge(x_step, X_STEPS * (b + 1))
                    if not (isinstance(b, int) and b == 0):
                        act.wait_ge(y_step, Y_STEPS * (b - 1) + 1)
                    nc.scalar.activation(nmy[:], nmx[:], ACT.Copy).then_inc(nmy_ok, 1)
                    act.wait_ge(nmy_ok, b + 1)
                wait(act, y_sq, n)
                nc.scalar.activation(junk[:], yc[s][:].rearrange("p k w -> p (k w)"), ACT.Square,
                                     bias=nmy[:], accum_out=ys2[:, j:j + 1]).then_inc(y_sq, 1)

            def totals(first, second, to_first, to_second, signal):
                nc.scalar.activation(first, first, ACT.Identity, scale=1.0 / CNT, accum_out=to_first)
                nc.scalar.activation(second, second, ACT.Identity, scale=1.0 / CNT,
                                     accum_out=to_second).then_inc(signal, 1)

            def x_totals(b):
                act.wait_ge(st_used, (b + 1) * STILES)
                totals(xs1[:], xs2[:], xn[:, M_REL], xn[:, V_SQ], x_tot)

            def y_totals(b):
                act.wait_ge(y_sq, (b + 1) * CHUNKS)
                totals(ys1[:], ys2[:], yn[:, M_LOC], yn[:, V_SQ], y_tot)

            def read(dst, src, count, func=ACT.Identity, **kw):
                act.wait_ge(small, count)
                nc.scalar.activation(dst, src, func, **kw).then_inc(small_rd, 1)

            def x_norm_read(i, count):
                read((mx, vx)[i][:], sm[:, (C_XM, C_XV)[i]:(C_XM, C_XV)[i] + 1], count)

            def off_bias(count):
                act.wait_ge(small, count)
                nc.scalar.activation(ob[:, 0:1], sm[:, C_OB:C_OB + 1], ACT.Identity, bias=bo[:, 0:1], scale=0.5)
                nc.scalar.activation(ob[:, 1:2], sm[:, C_OB + 1:C_OB + 2], ACT.Identity, bias=bo[:, 1:2],
                                     scale=0.5).then_inc(small_rd, 1)
                act.wait_ge(small_rd, count)

            act.wait_ge(loaded, LOADED)
            nc.scalar.activation(bo[:], bo[:], ACT.Copy, scale=0.5).then_inc(bo_half, 1)
            act.wait_ge(bo_half, 1)
            for i in range(STILES):
                x_sums(0, i)
            x_totals(0)
            x_norm_read(0, 1)
            x_norm_read(1, 2)
            off_bias(3)
            sides(0, 0)

            def step(b, j, own, nxt, prev, prev2):
                base = small_base(b)
                k = 4 if prev else 0
                dwc = dw_at(b, j, prev, prev2)
                if j == 1 and prev:
                    for y in y_at(b, j, own, prev):
                        y_square(*y)
                    y_totals(b - 1)
                    read(my[:], sm[:, C_YM:C_YM + 1], base + 1)
                if nxt and 0 < j <= STILES:
                    x_sums(b + 1, j - 1)
                    if j == STILES:
                        x_totals(b + 1)
                if j != 1:
                    for y in y_at(b, j, own, prev):
                        y_square(*y)
                if own:
                    offsets(b, j, 0)
                if j == 10 and nxt:
                    x_norm_read(0, base + k + (3 if prev else 2))
                if own:
                    offsets(b, j, 1)
                    if j in (0, CHUNKS - 1):
                        mirror_row(b, j)
                if j == 1 and prev:
                    read(vy[:], sm[:, C_YV:C_YV + 1], base + 2)
                if j == 10 and nxt:
                    x_norm_read(1, base + k + (4 if prev else 3))
                if j == 2 and prev:
                    read(wb[:], sm[:, C_WB:C_WB + 1], base + 5 + (1 if own else 0), bias=my[:])
                    act.wait_ge(small_rd, base + 5 + (1 if own else 0))
                if dwc:
                    finish(*dwc, 0)
                if j == 1 and prev:
                    read(hid[:], sm[0:HID, C_HID:C_HID + 1], base + 3, ACT.Relu, bias=b1c[:])
                if own and j < CHUNKS - 1:
                    sides(b, j + 1)
                elif nxt:
                    sides(b + 1, 0)
                if dwc:
                    finish(*dwc, 1)
                if j == 1 and prev:
                    read(tapr[:], sm[:, C_TAP:C_TAP + 6], base + 4)
                if j == 1 and own:
                    read(db[:], sm[:, C_DB:C_DB + 1], base + k + 1, bias=bd[:])
                if j == CHUNKS - 1 and nxt:
                    off_bias(base + k + (5 if prev else 4))

            all_steps(act, step)

        @block.vector
        def _(dve):
            def evacuate(b, j, h):
                n, s = cid(b, j), j % CS
                dve.wait_ge(dcn_mm, 2 * n + h + 1)
                if h == 0:
                    dve.wait_ge(y_in[s], ring_total(b, j, CS, lambda i: 1))
                    if j == 0:
                        dve.wait_ge(small_rd, small_base(b) + (1 if isinstance(b, int) and b == 0 else 5))
                        if not (isinstance(b, int) and b == 0):
                            dve.wait_ge(y_tot, b)
                y = yc[s][:, HALF * h:HALF * h + HALF, :].rearrange("p k w -> p (k w)")
                nc.vector.scalar_tensor_tensor(out=y, in0=dc[:, h, 0:NH], scalar=db[:], in1=y,
                                               op0=ALU.add, op1=ALU.add,
                                               accum_out=ys1[:, 2 * j + h:2 * j + h + 1])\
                    .then_inc(y_done, 1)

            def sample(b, j):
                n, s, v = cid(b, j), j % 2, xv[j % XS]
                at = n * LERPS
                q = nb[s]
                dve.wait_ge(sided, n + 1)
                wait_apart(dve, prepped, 4 * n + 1)
                if j in (0, CHUNKS - 1):
                    wait_apart(dve, mirror, 2 * b + 1 + (j > 0))
                m3 = mu[s][:].bitcast(U16).unsqueeze(1).to_broadcast([P, 3, NB, W])
                nc.vector.copy_predicated(q[:, :, :, 1:W - 1], m3[:, :, :, 1:W - 1],
                                          v[:, :, :, 3:W + 1]).then_inc(lerp, 1)
                m1 = mv[s][:].bitcast(U16)
                dve.wait_ge(lerp, at + 1)
                wait_apart(dve, prepped, 4 * n + 3)
                nc.vector.copy_predicated(v[:, ABOVE, :, 1:W + 1], m1, v[:, BELOW, :, 1:W + 1])
                nc.vector.copy_predicated(q[:, ABOVE], m1, q[:, BELOW]).then_inc(lerp, 1)
                pair = v[:, 0:2, :, 1:W + 1]
                u2 = du[s][:].unsqueeze(1).to_broadcast([P, 2, NB, W])
                dve.wait_ge(lerp, at + 2)
                nc.vector.tensor_tensor(q[:, 0:2], q[:, 0:2], pair, ALU.subtract).then_inc(lerp, 1)
                dve.wait_ge(lerp, at + 3)
                dve.wait_ge(prepped, 4 * n + 2)
                nc.vector.tensor_tensor(q[:, 0:2], q[:, 0:2], u2, ALU.mult).then_inc(lerp, 1)
                dve.wait_ge(lerp, at + 4)
                nc.vector.tensor_tensor(q[:, 0:2], q[:, 0:2], pair, ALU.add).then_inc(x_free, 1)
                dve.wait_ge(x_free, n + 1)
                nc.vector.tensor_tensor(q[:, 0], q[:, 0], q[:, 1], ALU.subtract).then_inc(lerp, 1)
                dve.wait_ge(lerp, at + 5)
                dve.wait_ge(prepped, 4 * n + 4)
                nc.vector.tensor_tensor(q[:, 0], q[:, 0], dv[s][:], ALU.mult).then_inc(lerp, 1)
                if j == 0:
                    nc.vector.tensor_copy(mxs[:], mx[:]).then_inc(mxs_ok, 1)
                    dve.wait_ge(mxs_ok, b + 1)
                pj = j - 2
                pb = b if pj >= 0 else b - 1
                if not (isinstance(pb, int) and pb < 0):
                    dve.wait_ge(s_sh[pj % CHUNKS % SS], ring_total(pb, pj % CHUNKS, SS, s_dmas))
                nc.vector.tensor_scalar(sc[s][:, :, 0:WP:WP - 1], zero[:, 0:2 * NB].rearrange(
                    "p (k e) -> p k e", e=2), mxs[:], None, ALU.add)
                if j == 0:
                    wait(dve, dcn_mm, 2 * (n - 2))
                    nc.vector.tensor_scalar(sa[0:C, 0, :], zero[0:C, 0:WP], mxs[0:C], None, ALU.add)
                if j == CHUNKS - 1:
                    dve.wait_ge(dcn_mm, 2 * (n - 2))
                    nc.vector.tensor_scalar(sw[P - C:P, SS * NB - 1, :], zero[P - C:P, 0:WP],
                                            mxs[P - C:P], None, ALU.add)
                dve.wait_ge(lerp, at + 6)
                nc.vector.tensor_tensor(sc[s][:, :, 1:W + 1], q[:, 0], q[:, 1], ALU.add)\
                    .then_inc(sampled, 1)

            dve.wait_ge(cleared, 6)

            def step(b, j, own, nxt, prev, prev2):
                if own:
                    sample(b, j)
                for d in dcn_at(b, j, own, prev):
                    for h in range(2):
                        evacuate(*d, h)

            all_steps(dve, step)

        @block.gpsimd
        def _(pool):
            ts, tt = nc.gpsimd.tensor_scalar, nc.gpsimd.tensor_tensor

            def pivot(b):
                wait_apart(pool, st_in[0], b * (16 * STILES // 2) + 16)
                ts(npiv[:], st[0][:, 0:1], -1.0, None, ALU.mult).then_inc(piv, 1)

            def x_norm(b, base):
                at = b * X_STEPS
                wait_apart(pool, x_tot, b + 1)
                tt(xn[:, M_LOC], xn[:, M_REL], npiv[:], ALU.subtract).then_inc(x_step, 1)
                tt(xn[:, M_SQ], xn[:, M_REL], xn[:, M_REL], ALU.mult).then_inc(x_step, 1)
                wait_apart(pool, x_step, at + 2)
                tt(xn[:, V_LOC], xn[:, V_SQ], xn[:, M_SQ], ALU.subtract).then_inc(x_step, 1)
                wait_apart(pool, small_rd, base + 1)
                ts(nmx[:], mx[:], -1.0, None, ALU.mult).then_inc(x_step, 1)
                wait_apart(pool, x_step, at + 4)
                tt(xn[:, DEV], xn[:, M_LOC], nmx[:], ALU.add).then_inc(x_step, 1)
                wait_apart(pool, x_step, at + 5)
                tt(xn[:, DEV_SQ], xn[:, DEV], xn[:, DEV], ALU.mult).then_inc(x_step, 1)
                wait_apart(pool, x_step, at + 6)
                tt(xn[:, V_ALL], xn[:, DEV_SQ], xn[:, V_LOC], ALU.add).then_inc(x_step, 1)
                wait_apart(pool, small_rd, base + 2)
                ts(xn[:, V_EPS], vx[:], EPS, None, ALU.add).then_inc(x_step, 1)
                wait_apart(pool, x_step, at + 8)
                tt(rx[:], xn[:, V_EPS], half[:], ALU.pow).then_inc(x_step, 1)
                wait_apart(pool, x_step, at + 9)

            def offset_weights(b):
                wait_apart(pool, off_mm, 2 * cid(b, 0))
                ts(wos[:], wo[:], rx[:], None, ALU.mult).then_inc(wo_ok, 1)

            def deform_weights(b):
                wait_apart(pool, dcn_mm, 2 * cid(b, 0))
                ts(wds[:], wd[:], rx[:], None, ALU.mult).then_inc(wd_ok, 1)

            def set_pads(b, j):
                n, v = cid(b, j), xv[j % XS]
                wait_apart(pool, off_mm, 2 * (n - XS + 1))
                if j == 0:
                    nc.gpsimd.tensor_copy(mxp[:], mx[:]).then_inc(mxp_ok, 1)
                    wait_apart(pool, mxp_ok, b + 1)
                if j in (0, CHUNKS - 1):
                    wait_apart(pool, x_free, n - XS + 1)
                    q, view, k = (slice(0, C), ABOVE, 0) if j == 0 else (slice(P - C, P), BELOW, NB - 1)
                    ts(v[q, view, k, 1:W + 1], zero[q, 0:W], mxp[q], None, ALU.add).then_inc(x_row, 1)
                    wait_apart(pool, x_row, 2 * b + (1 if j == 0 else 2))
                if j == CHUNKS - 1:
                    pool.sem_inc(pads, 1)
                    return
                for view in (ABOVE, BELOW):
                    last = ts(v[:, view, :, 0:WP:WP - 1],
                              zero[:, 0:2 * NB].rearrange("p (k e) -> p k e", e=2), mxp[:], None, ALU.add)
                last.then_inc(pads, 1)

            def y_norm(b, base):
                at = b * Y_STEPS
                wait_apart(pool, y_tot, b + 1)
                tt(yn[:, M_REL], yn[:, M_LOC], nmy[:], ALU.add).then_inc(y_step, 1)
                wait_apart(pool, y_step, at + 1)
                tt(yn[:, M_SQ], yn[:, M_REL], yn[:, M_REL], ALU.mult).then_inc(y_step, 1)
                wait_apart(pool, y_step, at + 2)
                tt(yn[:, V_LOC], yn[:, V_SQ], yn[:, M_SQ], ALU.subtract).then_inc(y_step, 1)
                wait_apart(pool, small_rd, base + 1)
                ts(my_neg[:], my[:], -1.0, None, ALU.mult).then_inc(y_step, 1)
                wait_apart(pool, y_step, at + 4)
                tt(yn[:, DEV], yn[:, M_LOC], my_neg[:], ALU.add).then_inc(y_step, 1)
                wait_apart(pool, y_step, at + 5)
                tt(yn[:, DEV_SQ], yn[:, DEV], yn[:, DEV], ALU.mult).then_inc(y_step, 1)
                wait_apart(pool, y_step, at + 6)
                tt(yn[:, V_ALL], yn[:, DEV_SQ], yn[:, V_LOC], ALU.add).then_inc(y_step, 1)
                wait_apart(pool, small_rd, base + 2)
                ts(yn[:, V_EPS], vy[:], EPS, None, ALU.add).then_inc(y_step, 1)
                wait_apart(pool, y_step, at + 8)
                tt(ry[:], yn[:, V_EPS], half[:], ALU.pow).then_inc(y_step, 1)
                wait_apart(pool, y_step, at + 9)
                tt(yn[:, D_STD], yn[:, DEV], ry[:], ALU.mult).then_inc(y_step, 1)
                wait_apart(pool, y_step, at + 10)
                ts(pooled[:], yn[:, D_STD], 1.0 / G, None, ALU.mult).then_inc(y_step, 1)
                wait_apart(pool, small_rd, base + 4)
                tt(tap[:], tapr[:], b2r[:], ALU.add).then_inc(y_step, 1)
                wait_apart(pool, y_step, at + 12)
                ts(tap[:], tap[:], ry[:], None, ALU.mult).then_inc(y_step, 1)
                wait_apart(pool, y_step, at + 13)
                tt(tap[:], tap[:], kc[:, K_CEN], ALU.add).then_inc(y_step, 1)
                wait_apart(pool, y_step, at + 14)
                wait_apart(pool, dw_mm, 2 * cid(b, 0))
                tt(wy[:].rearrange("p t (o c) -> p o t c", o=2),
                   kc[:, K_EYE].unsqueeze(1).unsqueeze(1).to_broadcast([P, 2, 3, C]),
                   tap[:].rearrange("p (o t) -> p o t", o=2).unsqueeze(3).to_broadcast([P, 2, 3, C]),
                   ALU.mult)
                edges = zero[:, 0:2 * BLOCKS].rearrange("p (k e) -> p k e", e=2)
                ts(ya[:, :, 0:WP:WP - 1], edges, my[:], None, ALU.add)
                ts(yb[:, :, 0:WP:WP - 1], edges, my[:], None, ALU.add).then_inc(y_row, 1)
                wait_apart(pool, y_row, 3 * b + 1)
                ts(ya[0:C, 0, 1:W + 1], zero[0:C, 0:W], my[0:C], None, ALU.add).then_inc(y_row, 1)
                wait_apart(pool, y_row, 3 * b + 2)
                q = slice(P - C, P)
                ts(yb[q, BLOCKS - 1, 1:W + 1], zero[q, 0:W], my[q], None, ALU.add).then_inc(y_row, 1)
                wait_apart(pool, y_row, 3 * b + 3)
                pool.sem_inc(wy_ok, 1)

            for tile in (wo, wd, w2r, b2r, zero):
                nc.gpsimd.memset(tile[:], 0.0).then_inc(cleared, 1)
            nc.gpsimd.memset(half[:], -0.5).then_inc(cleared, 1)
            pool.wait_ge(cleared, 6)
            pool.wait_ge(loaded, LOADED)
            pivot(0)
            x_norm(0, 0)
            set_pads(0, 0)
            offset_weights(0)

            def step(b, j, own, nxt, prev, prev2):
                base = small_base(b)
                if j == 0:
                    if nxt:
                        pivot(b + 1)
                    if own:
                        set_pads(b, 1)
                        set_pads(b, 2)
                        deform_weights(b)
                if j == 1 and prev:
                    y_norm(b - 1, base)
                if j == 9 and nxt:
                    x_norm(b + 1, base + (6 if prev else 1))
                if j == 10 and own:
                    set_pads(b, CHUNKS - 1)
                if j == 11 and nxt:
                    set_pads(b + 1, 0)
                    offset_weights(b + 1)

            all_steps(pool, step)


def kernel(x, L0_conv_w_off, L0_conv_b_off, L0_conv_w_dcn, L0_conv_b_dcn, L1_conv_w1, L1_conv_b1,
           L1_conv_w2, L1_conv_b2):
    import concourse.bacc as bacc
    from concourse.bass_utils import run_bass_kernel_spmd

    p = np.arange(P)
    consts = np.zeros((P, P + C + 6), np.float32)
    consts[:, K_AVG] = (p[:, None] % C // 2 == p[None, :] % C // 2) / (2.0 * G)
    consts[:, K_EYE] = p[:, None] % C == np.arange(C)[None, :]
    for o in range(2):
        consts[:, P + C + 3 * o + 1] = p // C - o == 1
    asc = np.ascontiguousarray
    arrays = {
        "x": asc(np.asarray(x).transpose(0, 2, 1, 3)),
        "w_off": asc(np.asarray(L0_conv_w_off).reshape(C, 2, C, 3, 3).transpose(3, 1, 2, 4, 0)),
        "b_off": asc(np.asarray(L0_conv_b_off).reshape(C, 2)),
        "w_dcn": asc(np.asarray(L0_conv_w_dcn).transpose(2, 1, 3, 0)),
        "b_dcn": asc(np.asarray(L0_conv_b_dcn).reshape(C, 1)),
        "w1": asc(L1_conv_w1),
        "b1": asc(np.asarray(L1_conv_b1).reshape(HID, 1)),
        "w2": asc(np.asarray(L1_conv_w2).reshape(HID, C, 3, 3).transpose(2, 0, 3, 1)),
        "b2": asc(np.asarray(L1_conv_b2).reshape(C, 3, 3).transpose(1, 0, 2)),
        "consts": consts,
    }
    nc = bacc.Bacc("TRN2", target_bir_lowering=False, num_devices=1)
    maps = {f"in_{name}": a for name, a in arrays.items()}
    args = [nc.dram_tensor(name, a.shape, mybir.dt.from_np(a.dtype), kind="ExternalInput").ap()
            for name, a in maps.items()]
    out = nc.dram_tensor("out", (B, H, C, W), F32, kind="ExternalOutput").ap()
    block_kernel(nc, *args, out)
    got = run_bass_kernel_spmd(nc, [maps], core_ids=[0]).results[0]["out"]
    return asc(np.asarray(got).transpose(0, 2, 1, 3))
```

```python
from contextlib import ExitStack

import numpy as np

import concourse.bass as bass
from concourse import mybir

F32 = mybir.dt.float32
BF16 = mybir.dt.bfloat16
U16 = mybir.dt.uint16
ALU = mybir.AluOpType
ACT = mybir.ActivationFunctionType

P = 128
C = 32
G = P // C
B, H, W = 8, 192, 192
HW = H * W
WP = W + 2
NB = 4
CHUNKS = H // (G * NB)
HALF = NB // 2
N = NB * W
NH = HALF * W
BLOCKS = H // G
HID = 64
EPS = 1e-5
CNT = HW // G
STILES = 8
SBLOCKS = BLOCKS // STILES
SW = SBLOCKS * W
XS, SS, CS = 3, 3, 4
ABOVE, MID, BELOW = 0, 1, 2
BANK = 512
K_AVG, K_EYE, K_CEN = slice(0, P), slice(P, P + C), slice(P + C, P + C + 6)
M_REL, M_SQ, M_LOC, V_SQ, V_LOC, DEV, DEV_SQ, V_ALL, V_EPS, D_STD = (
    slice(i, i + 1) for i in range(10))
C_XM, C_XV, C_OB, C_DB, C_YM, C_YV, C_HID, C_TAP, C_WB = 0, 1, 2, 4, 5, 6, 7, 8, 14
BANDS = [(g, o) for o in range(2) for g in range(G) if 0 <= g - o <= 2]
LOADED = 16 * 9
X_STEPS, Y_STEPS = 9, 14
LERPS = 9
PADDED = 4


def x_dmas(j):
    return 3 + (j in (0, CHUNKS - 1))


def s_dmas(j):
    return 4 + (j % SS == SS - 1 and j != CHUNKS - 1) + (j % SS == 0 and j != 0)


def ring_total(b, j, slots, dmas):
    mine = range(j % slots, CHUNKS, slots)
    return b * (16 * sum(dmas(i) for i in mine)) + 16 * sum(dmas(i) for i in mine if i <= j)


def ring_before(b, j, slots, dmas):
    return ring_total(b, j, slots, dmas) - 16 * dmas(j)


def wait(eng, sem, value):
    if not isinstance(value, int) or value > 0:
        eng.wait_ge(sem, value)


def pads_set(b, j):
    return PADDED * b + (min(j, 2) + 1 if j < CHUNKS - 1 else PADDED)


def small_base(b):
    if isinstance(b, int):
        if b == 0:
            return 3
        if b == B:
            return 7 + 9 * (B - 2) + 6
    return (b - 1) * 9 + 7


def bias_read(b):
    return small_base(b) + (1 if isinstance(b, int) and b == 0 else 4)


def block_kernel(nc, x, planes, w_off, b_off, w_dcn, b_dcn, w1, b1, w2, b2, consts, out):
    with ExitStack() as ctx:
        def sb(name, shape, dt=F32):
            return ctx.enter_context(nc.sbuf_tensor(name, shape, dt))

        def sem(name):
            return ctx.enter_context(nc.semaphore(name))

        xv = [sb(f"xv{s}", [P, 3, NB, WP]) for s in range(XS)]
        nb = [sb(f"nb{s}", [P, 3, NB, W]) for s in range(2)]
        du = [sb(f"du{s}", [P, NB, W]) for s in range(2)]
        dv = [sb(f"dv{s}", [P, NB, W]) for s in range(2)]
        mu = [sb(f"mu{s}", [P, NB, W], BF16) for s in range(2)]
        mv = [sb(f"mv{s}", [P, NB, W], BF16) for s in range(2)]
        sc = [sb(f"sc{s}", [P, NB, WP]) for s in range(2)]
        sa = sb("sa", [P, SS * NB, WP])
        sw = sb("sw", [P, SS * NB, WP])
        yc = [sb(f"yc{s}", [P, NB, W]) for s in range(CS)]
        ya = sb("ya", [P, BLOCKS, WP])
        yb = sb("yb", [P, BLOCKS, WP])
        ot = [sb(f"ot{s}", [P, NB, W]) for s in range(2)]
        st = [sb(f"st{s}", [P, SW]) for s in range(2)]
        junk = sb("junk", [P, N], BF16)
        wo = sb("wo", [P, 2, 3, 2 * C])
        wos = sb("wos", [P, 2, 3, 2 * C])
        wd = sb("wd", [P, 3, 2 * C])
        wds = sb("wds", [P, 3, 2 * C])
        wy = sb("wy", [P, 3, 2 * C])
        w1r = sb("w1r", [P, HID])
        w2r = sb("w2r", [HID, 6, P])
        b2r = sb("b2r", [P, 6])
        b1c = sb("b1c", [HID, 1])
        bo = sb("bo", [P, 2])
        bd = sb("bd", [P, 1])
        kc = sb("kc", [P, P + C + 6])
        zero = sb("zero", [P, 2 * WP])
        xs1 = sb("xs1", [P, STILES])
        xs2 = sb("xs2", [P, STILES])
        ys1 = sb("ys1", [P, 2 * CHUNKS])
        ys2 = sb("ys2", [P, CHUNKS])
        xn = sb("xn", [P, 16])
        yn = sb("yn", [P, 16])
        half = sb("half", [P, 1])
        npiv = sb("npiv", [P, 1])
        mx = sb("mx", [P, 1])
        vx = sb("vx", [P, 1])
        rx = sb("rx", [P, 1])
        nmx = sb("nmx", [P, 1])
        mxs = sb("mxs", [P, 1])
        mxp = sb("mxp", [P, 1])
        nmy = sb("nmy", [P, 1])
        my = sb("my", [P, 1])
        vy = sb("vy", [P, 1])
        ry = sb("ry", [P, 1])
        my_neg = sb("my_neg", [P, 1])
        pooled = sb("pooled", [P, 1])
        hid = sb("hid", [HID, 1])
        tapr = sb("tapr", [P, 6])
        tap = sb("tap", [P, 6])
        ob = sb("ob", [P, 2])
        db = sb("db", [P, 1])
        wb = sb("wb", [P, 1])

        z = ctx.enter_context(nc.psum_tensor("z", [P, 2, 2, BANK], F32))
        dc = ctx.enter_context(nc.psum_tensor("dc", [P, 2, BANK], F32))
        dw = ctx.enter_context(nc.psum_tensor("dw", [P, BANK], F32))
        sm = ctx.enter_context(nc.psum_tensor("sm", [P, BANK], F32))

        loaded = sem("loaded")
        cleared = sem("cleared")
        x_in = [sem(f"x_in{s}") for s in range(XS)]
        st_in = [sem(f"st_in{s}") for s in range(2)]
        first_in = [sem(f"first_in{i}") for i in range(STILES)]
        first_sum = sem("first_sum")
        y_in = [sem(f"y_in{s}") for s in range(CS)]
        s_sh = [sem(f"s_sh{s}") for s in range(SS)]
        y_sh = [sem(f"y_sh{s}") for s in range(CS)]
        o_out = [sem(f"o_out{s}") for s in range(2)]
        piv = sem("piv")
        centred = sem("centred")
        bo_half = sem("bo_half")
        st_used = sem("st_used")
        x_row = sem("x_row")
        y_row = sem("y_row")
        pads = sem("pads")
        off_mm = sem("off_mm")
        z_read = sem("z_read")
        mirror = sem("mirror")
        sided = sem("sided")
        prepped = sem("prepped")
        lerp = sem("lerp")
        x_free = sem("x_free")
        sampled = sem("sampled")
        dcn_mm = sem("dcn_mm")
        y_done = sem("y_done")
        y_sq = sem("y_sq")
        dw_mm = sem("dw_mm")
        o_done = sem("o_done")
        small = sem("small")
        small_rd = sem("small_rd")
        x_tot = sem("x_tot")
        y_tot = sem("y_tot")
        x_step = sem("x_step")
        y_step = sem("y_step")
        wo_ok = sem("wo_ok")
        wd_ok = sem("wd_ok")
        wy_ok = sem("wy_ok")
        mxs_ok = sem("mxs_ok")
        mxp_ok = sem("mxp_ok")
        nmy_ok = sem("nmy_ok")
        passed = sem("passed")
        block = ctx.enter_context(nc.Block())

        lines = x.rearrange("b h c w -> b (h c) w")
        parts = planes.rearrange("b c (g i r) w -> b i g c (r w)", g=G, i=STILES)

        def blocks_of(t, b, first, count):
            return t[b, first:first + P * count, :].rearrange("(k p) w -> p k w", p=P)

        def wait_apart(eng, sem, value):
            if not isinstance(value, int):
                eng.wait_ge(sem, value)
                eng.sem_inc(passed, 1)
            elif value > 0:
                eng.wait_ge(sem, value)

        def cid(b, j):
            return b * CHUNKS + j

        def first_tile(t, i):
            return t[:].rearrange("p k w -> p (k w)")[:, SW * i:SW * (i + 1)]

        def two_banks(b):
            return isinstance(b, int) and b == B - 1

        def dw_bank(b, j, h):
            return dc[:, h, 0:NH] if two_banks(b) or j == CHUNKS - 1 and h else dw[:, 0:NH]

        def all_steps(eng, step):
            def image(b, last, own, nxt, prev, prev2):
                for j in range(last):
                    step(b, j, own, nxt, prev, prev2)
            image(0, CHUNKS, True, True, False, False)
            image(1, CHUNKS, True, True, True, False)
            with eng.Fori(2, B - 1) as b:
                image(b, CHUNKS, True, True, True, True)
            image(B - 1, CHUNKS, True, False, True, True)
            image(B, CHUNKS, False, False, True, True)
            image(B + 1, 2, False, False, False, True)

        def dw_at(b, j, prev, prev2):
            if j >= 2:
                return (b - 1, j - 2) if prev else None
            return (b - 2, CHUNKS - 2 + j) if prev2 else None

        def dcn_at(b, j, own, prev):
            if j >= 2:
                return [(b, j - 2)] if own else []
            if j == 0 and prev:
                return [(b - 1, CHUNKS - 2), (b - 1, CHUNKS - 1)]
            return []

        def y_at(b, j, own, prev):
            if j >= 3:
                return [(b, j - 3)] if own else []
            if j == 0 and prev:
                return [(b - 1, CHUNKS - 3)]
            if j == 1 and prev:
                return [(b - 1, CHUNKS - 2), (b - 1, CHUNKS - 1)]
            return []

        @block.sync
        def _(sp):
            def x_load(b, j):
                s, k = j % XS, j * NB
                n = cid(b, j)
                wait_apart(sp, x_free, n - XS + 1)
                pj = j - XS
                pb = b if pj >= 0 else b - 1
                if not (isinstance(pb, int) and pb < 0):
                    wait_apart(sp, y_in[pj % CS], ring_total(pb, pj % CHUNKS, CS, lambda i: 1))
                v, done = xv[s], x_in[s]
                for view in range(3):
                    line, k0, k1 = P * k + C * (view - 1), 0, NB
                    if j == 0 and view == ABOVE:
                        sp.dma_start(v[C:P, view, 0, 1:W + 1], lines[b, 0:P - C, :]).then_inc(done, 16)
                        k0 = 1
                    if j == CHUNKS - 1 and view == BELOW:
                        sp.dma_start(v[0:P - C, view, NB - 1, 1:W + 1], lines[b, H * C - P + C:H * C, :])\
                            .then_inc(done, 16)
                        k1 = NB - 1
                    sp.dma_start(v[:, view, k0:k1, 1:W + 1],
                                 blocks_of(lines, b, line + P * k0, k1 - k0)).then_inc(done, 16)

            def st_load(b, i):
                wait_apart(sp, st_used, b * STILES + i - 1)
                if isinstance(b, int) and b == 1 and i == 0:
                    sp.wait_ge(first_sum, STILES)
                sp.dma_start(st[i % 2][:], parts[b, i]).then_inc(st_in[i % 2], 16)

            def residual(b, j):
                s = j % CS
                n = cid(b, j)
                wait_apart(sp, x_in[j % XS], ring_total(b, j, XS, x_dmas))
                wait_apart(sp, y_sh[s], ring_before(b, j, CS, lambda i: 4))
                wait_apart(sp, y_sq, n - CS + 1)
                sp.dma_start(yc[s][:], xv[j % XS][:, MID, :, 1:W + 1]).then_inc(y_in[s], 16)

            def s_shift(b, j):
                n, s, k = cid(b, j), j % SS, (j % SS) * NB
                q, done = sc[j % 2], s_sh[j % SS]
                wait_apart(sp, sampled, n + 1)
                wait_apart(sp, dcn_mm, 2 * (n - 1))
                sp.dma_start(sa[C:P, k:k + NB, :], q[0:P - C, :, :]).then_inc(done, 16)
                sp.dma_start(sw[0:P - C, k:k + NB, :], q[C:P, :, :]).then_inc(done, 16)
                top, bottom = slice(0, C), slice(P - C, P)
                if s == SS - 1:
                    sp.dma_start(sa[top, k + 1:k + NB, :], q[bottom, 0:NB - 1, :]).then_inc(done, 16)
                    if j != CHUNKS - 1:
                        sp.dma_start(sa[top, 0:1, :], q[bottom, NB - 1:NB, :]).then_inc(done, 16)
                else:
                    sp.dma_start(sa[top, k + 1:k + NB + 1, :], q[bottom, :, :]).then_inc(done, 16)
                if s == 0:
                    sp.dma_start(sw[bottom, 0:NB - 1, :], q[top, 1:NB, :]).then_inc(done, 16)
                    if j != 0:
                        sp.dma_start(sw[bottom, SS * NB - 1:SS * NB, :], q[top, 0:1, :]).then_inc(done, 16)
                else:
                    sp.dma_start(sw[bottom, k - 1:k + NB - 1, :], q[top, :, :]).then_inc(done, 16)

            def y_shift(b, j):
                n, k, q, done = cid(b, j), j * NB, yc[j % CS], y_sh[j % CS]
                wait_apart(sp, y_done, 2 * (n + 1))
                wait_apart(sp, dw_mm, 2 * cid(b - 1, j + 1) + (j < CHUNKS - 1))
                sp.dma_start(ya[C:P, k:k + NB, 1:W + 1], q[0:P - C]).then_inc(done, 16)
                sp.dma_start(yb[0:P - C, k:k + NB, 1:W + 1], q[C:P]).then_inc(done, 16)
                top, bottom = slice(0, C), slice(P - C, P)
                m = NB - (j == CHUNKS - 1)
                sp.dma_start(ya[top, k + 1:k + 1 + m, 1:W + 1], q[bottom, 0:m]).then_inc(done, 16)
                m = int(j == 0)
                sp.dma_start(yb[bottom, k + m - 1:k + NB - 1, 1:W + 1], q[top, m:NB]).then_inc(done, 16)

            def store(b, j):
                n, s = cid(b, j), j % 2
                wait_apart(sp, o_done, 2 * (n + 1))
                sp.dma_start(out[b, :, NB * j:NB * j + NB, :], ot[s][:]).then_inc(o_out[s], 16)

            weights = ((kc, consts), (wo, w_off), (bo, b_off), (wd, w_dcn), (bd, b_dcn), (w1r, w1),
                       (b1c, b1), (w2r, w2), (b2r, b2))
            for i in range(max(STILES, len(weights))):
                if i < STILES:
                    sp.dma_start(first_tile(ya, i), parts[0, i])\
                        .then_inc(first_in[i], 16)
                if i < len(weights):
                    sp.dma_start(weights[i][0][:], weights[i][1]).then_inc(loaded, 16)
            x_load(0, 0)

            def step(b, j, own, nxt, prev, prev2):
                if own and j < CHUNKS - 1:
                    x_load(b, j + 1)
                if nxt and j == CHUNKS - 1:
                    x_load(b + 1, 0)
                if nxt and j < STILES:
                    st_load(b + 1, j)
                if own:
                    residual(b, j)
                before = dw_at(b, j - 1, prev, prev2) if j else (
                    (b - 2, CHUNKS - 3) if prev2 else None)
                if j:
                    if own:
                        s_shift(b, j - 1)
                elif prev:
                    s_shift(b - 1, CHUNKS - 1)
                if before:
                    store(*before)
                for y in y_at(b, j, own, prev):
                    y_shift(*y)

            all_steps(sp, step)
            store(B - 1, CHUNKS - 1)
            for s in range(2):
                sp.wait_ge(o_out[s], 16 * B * CHUNKS // 2)

        @block.tensor
        def _(pe):
            halves = (slice(0, 2 * C), slice(2 * C, P))

            def conv(acc, weights, above, below):
                for kx in range(3):
                    for m, view in zip(halves, (above, below)):
                        last = nc.tensor.matmul(acc[m, :], weights[:, kx, :], view[:, :, kx:kx + W],
                                                start=kx == 0, stop=kx == 2)
                return last

            def offsets(b, j, i):
                n, s = cid(b, j), j % XS
                if i == 0:
                    pe.wait_ge(x_in[s], ring_total(b, j, XS, x_dmas))
                    pe.wait_ge(pads, pads_set(b, j))
                    if j == 0:
                        pe.wait_ge(wo_ok, b + 1)
                wait(pe, z_read, 2 * (n - 1) + i + 1)
                for h in range(2):
                    k = slice(HALF * h, HALF * h + HALF)
                    last = conv(z[:, i, h, 0:NH], wos[:, i], xv[s][:, ABOVE, k, :], xv[s][:, BELOW, k, :])
                last.then_inc(off_mm, 1)

            def deform(b, j, h):
                n, k = cid(b, j), (j % SS) * NB + HALF * h
                if h == 0:
                    if j == 0:
                        pe.wait_ge(wd_ok, b + 1)
                        pe.wait_ge(small_rd, bias_read(b))
                    for i in (j - 1, j, j + 1):
                        if 0 <= i < CHUNKS:
                            pe.wait_ge(s_sh[i % SS], ring_total(b, i, SS, s_dmas))
                    pe.wait_ge(sampled, cid(b, min(j + 1, CHUNKS - 1)) + 1)
                wait(pe, y_done, 2 * (n - 1) + h + 1)
                conv(dc[:, h, 0:NH], wds, sa[:, k:k + HALF, :], sw[:, k:k + HALF, :]).then_inc(dcn_mm, 1)

            def depthwise(b, j, h):
                n, k = cid(b, j), j * NB + HALF * h
                if h == 0 and j == 0:
                    pe.wait_ge(wy_ok, b + 1)
                    for i in range(CHUNKS - CS, CHUNKS):
                        pe.wait_ge(y_sh[i % CS], ring_total(b, i, CS, lambda i: 4))
                wait(pe, o_done, 2 * n + h - (two_banks(b) or j == CHUNKS - 1 and h == 1))
                conv(dw_bank(b, j, h), wy, ya[:, k:k + HALF, :], yb[:, k:k + HALF, :]).then_inc(dw_mm, 1)

            def average(col, src, count):
                wait(pe, small_rd, count)
                nc.tensor.matmul(sm[:, col:col + 1], kc[:, K_AVG], src, start=True, stop=True)\
                    .then_inc(small, 1)

            def biases(cols, sets, mean, count, bank=sm):
                wait(pe, small_rd, count)
                for col, weights in zip(cols, sets):
                    for kx in range(3):
                        for m in halves:
                            last = nc.tensor.matmul(bank[m, col:col + 1], weights[:, kx, :], mean,
                                                    start=kx == 0, stop=kx == 2)
                last.then_inc(small, 1)

            pe.wait_ge(loaded, LOADED)

            def x_norm_mm(b, i, base):
                pe.wait_ge(x_step, X_STEPS * b + (1, 7)[i])
                average((C_XM, C_XV)[i], (xn[:, M_LOC], xn[:, V_ALL])[i], base + i)

            x_norm_mm(0, 0, 0)
            x_norm_mm(0, 1, 0)
            pe.wait_ge(wo_ok, 1)
            biases((C_OB, C_OB + 1), (wos[:, 0], wos[:, 1]), nmx[:], 2)

            def step(b, j, own, nxt, prev, prev2):
                base = small_base(b)
                k = 4 if prev else 0
                dwc, dcs = dw_at(b, j, prev, prev2), dcn_at(b, j, own, prev)
                if own:
                    offsets(b, j, 0)
                if j == 2 and prev:
                    pe.wait_ge(small_rd, base + 3)
                    wait(pe, small_rd, base + (4 if own else 3))
                    for t in range(6):
                        last = nc.tensor.matmul(sm[:, C_TAP + t:C_TAP + t + 1], w2r[:, t, :], hid[:],
                                                start=True, stop=True)
                    last.then_inc(small, 1)
                if j == 10 and nxt:
                    x_norm_mm(b + 1, 0, base + k + (2 if prev else 1))
                if own:
                    offsets(b, j, 1)
                if j == 1 and prev:
                    pe.wait_ge(y_tot, b)
                    average(C_YM, yn[:, M_LOC], base)
                if j == 2 and prev:
                    pe.wait_ge(wy_ok, b)
                    biases((C_WB,), (wy,), my_neg[:], base + 4 + (1 if own else 0))
                early = j == 0 and not own
                if early and dwc:
                    for h in range(2):
                        depthwise(*dwc, h)
                for h in range(2):
                    if dwc and not early:
                        depthwise(*dwc, h)
                    if j == 1 and prev and h == 0:
                        pe.wait_ge(y_step, Y_STEPS * (b - 1) + 7)
                        average(C_YV, yn[:, V_ALL], base + 1)
                    if j == 10 and nxt and h == 0:
                        x_norm_mm(b + 1, 1, base + k + (2 if prev else 1))
                    for d in dcs[:1]:
                        deform(*d, h)
                for d in dcs[1:]:
                    for h in range(2):
                        deform(*d, h)
                if j == 1 and prev:
                    pe.wait_ge(y_step, Y_STEPS * (b - 1) + 11)
                    wait(pe, small_rd, base + 2)
                    nc.tensor.matmul(sm[0:HID, C_HID:C_HID + 1], w1r[:], pooled[:],
                                     start=True, stop=True).then_inc(small, 1)
                if j == 1 and own:
                    pe.wait_ge(wd_ok, b + 1)
                    biases((C_DB,), (wds,), nmx[:], base + (2 if prev else 0), dc[:, 0, :])
                if j == CHUNKS - 1 and nxt:
                    pe.wait_ge(wo_ok, b + 2)
                    biases((C_OB, C_OB + 1), (wos[:, 0], wos[:, 1]), nmx[:],
                           base + k + (4 if prev else 3))

            all_steps(pe, step)

        @block.scalar
        def _(act):
            def offsets(b, j, i):
                n, s = cid(b, j), j % 2
                d, m = ((du, mu), (dv, mv))[i]
                act.wait_ge(off_mm, 2 * n + i + 1)
                wait(act, sampled, n - 1)
                nc.scalar.activation(d[s][:].rearrange("p (h k) w -> p h (k w)", h=2),
                                     z[:, i, :, 0:NH], ACT.Tanh, bias=ob[:, i:i + 1], scale=0.5)\
                    .then_inc(z_read, 1)
                act.wait_ge(z_read, 2 * n + i + 1)
                nc.scalar.activation(m[s][:], d[s][:], ACT.Relu, scale=-1.0).then_inc(prepped, 1)
                if i == 1 and j in (0, CHUNKS - 1):
                    mirror_row(b, j)
                nc.scalar.activation(d[s][:], d[s][:], ACT.Abs, scale=0.5).then_inc(prepped, 1)

            def sides(b, j):
                n, s, v = cid(b, j), j % 2, xv[j % XS]
                act.wait_ge(x_in[j % XS], ring_total(b, j, XS, x_dmas))
                act.wait_ge(pads, pads_set(b, j))
                wait(act, sampled, n - 1)
                nc.scalar.activation(nb[s][:, :, :, 1:W], v[:, :, :, 1:W], ACT.Copy)
                nc.scalar.activation(nb[s][:, :, :, 0:1], v[:, :, :, 2:3], ACT.Copy).then_inc(sided, 1)

            def mirror_row(b, j):
                q, k = (slice(0, C), 0) if j == 0 else (slice(P - C, P), NB - 1)
                act.wait_ge(prepped, 4 * cid(b, j) + 3)
                kw = dict(func=ACT.Identity, bias=half[q]) if j == 0 else dict(func=ACT.Copy)
                nc.scalar.activation(out=mv[j % 2][q, k, :], in_=zero[q, 0:W], **kw).then_inc(mirror, 1)

            def finish(b, j, h):
                n, s = cid(b, j), j % 2
                act.wait_ge(dw_mm, 2 * n + h + 1)
                if h == 0:
                    pj = j - 2
                    pb = b if pj >= 0 else b - 1
                    if not (isinstance(pb, int) and pb < 0):
                        act.wait_ge(o_out[s], ring_total(pb, pj % CHUNKS, 2, lambda i: 1))
                nc.scalar.activation(ot[s][:, HALF * h:HALF * h + HALF, :].rearrange("p k w -> p (k w)"),
                                     dw_bank(b, j, h), ACT.Identity, bias=wb[:]).then_inc(o_done, 1)

            def x_sums(b, i):
                s = i % 2
                act.wait_ge(st_in[s], (b - 1) * (16 * STILES // 2) + 16 * (i // 2 + 1))
                if i == 0:
                    act.wait_ge(piv, b + 1)
                nc.scalar.activation(st[s][:], st[s][:], ACT.Identity, bias=npiv[:],
                                     accum_out=xs1[:, i:i + 1]).then_inc(centred, 1)
                act.wait_ge(centred, (b - 1) * STILES + i + 1)
                nc.scalar.activation(st[s][:], st[s][:], ACT.Square,
                                     accum_out=xs2[:, i:i + 1]).then_inc(st_used, 1)

            def y_square(b, j):
                n, s = cid(b, j), j % CS
                act.wait_ge(y_done, 2 * (n + 1))
                if j == 0:
                    act.wait_ge(x_step, X_STEPS * (b + 1))
                    if not (isinstance(b, int) and b == 0):
                        act.wait_ge(y_step, Y_STEPS * (b - 1) + 1)
                    nc.scalar.activation(nmy[:], nmx[:], ACT.Copy).then_inc(nmy_ok, 1)
                    act.wait_ge(nmy_ok, b + 1)
                wait(act, y_sq, n)
                nc.scalar.activation(junk[:], yc[s][:].rearrange("p k w -> p (k w)"), ACT.Square,
                                     bias=nmy[:], accum_out=ys2[:, j:j + 1]).then_inc(y_sq, 1)

            def totals(first, second, to_first, to_second, signal):
                nc.scalar.activation(first, first, ACT.Identity, scale=1.0 / CNT, accum_out=to_first)
                nc.scalar.activation(second, second, ACT.Identity, scale=1.0 / CNT,
                                     accum_out=to_second).then_inc(signal, 1)

            def x_totals(b):
                act.wait_ge(st_used, (b + 1) * STILES)
                totals(xs1[:], xs2[:], xn[:, M_REL], xn[:, V_SQ], x_tot)

            def y_totals(b):
                act.wait_ge(y_sq, (b + 1) * CHUNKS)
                totals(ys1[:], ys2[:], yn[:, M_LOC], yn[:, V_SQ], y_tot)

            def read(dst, src, count, func=ACT.Identity, **kw):
                act.wait_ge(small, count)
                nc.scalar.activation(dst, src, func, **kw).then_inc(small_rd, 1)

            def x_norm_read(i, count):
                read((mx, vx)[i][:], sm[:, (C_XM, C_XV)[i]:(C_XM, C_XV)[i] + 1], count)

            def off_bias(count):
                act.wait_ge(small, count)
                nc.scalar.activation(ob[:, 0:1], sm[:, C_OB:C_OB + 1], ACT.Identity, bias=bo[:, 0:1], scale=0.5)
                nc.scalar.activation(ob[:, 1:2], sm[:, C_OB + 1:C_OB + 2], ACT.Identity, bias=bo[:, 1:2],
                                     scale=0.5).then_inc(small_rd, 1)
                act.wait_ge(small_rd, count)

            act.wait_ge(piv, 1)
            for i in range(STILES):
                act.wait_ge(first_in[i], 16)
                nc.scalar.activation(first_tile(yb, i), first_tile(ya, i), ACT.Square, bias=npiv[:],
                                     accum_out=xs2[:, i:i + 1]).then_inc(st_used, 1)
            act.wait_ge(first_sum, STILES)
            x_totals(0)
            act.wait_ge(loaded, LOADED)
            nc.scalar.activation(bo[:], bo[:], ACT.Copy, scale=0.5).then_inc(bo_half, 1)
            act.wait_ge(bo_half, 1)
            x_norm_read(0, 1)
            x_norm_read(1, 2)
            off_bias(3)
            sides(0, 0)

            def step(b, j, own, nxt, prev, prev2):
                base = small_base(b)
                k = 4 if prev else 0
                dwc = dw_at(b, j, prev, prev2)
                late = j == 1 and prev
                ys = y_at(b, j, own, prev)
                if nxt and 0 < j <= STILES:
                    x_sums(b + 1, j - 1)
                    if j == STILES:
                        x_totals(b + 1)
                if own:
                    offsets(b, j, 0)
                for y in ys:
                    y_square(*y)
                if late:
                    y_totals(b - 1)
                    read(my[:], sm[:, C_YM:C_YM + 1], base + 1)
                if j == 2 and prev:
                    read(tapr[:], sm[:, C_TAP:C_TAP + 6], base + 4 + own)
                if j == 10 and nxt:
                    x_norm_read(0, base + k + (3 if prev else 2))
                if own:
                    offsets(b, j, 1)
                if j == 2 and prev:
                    read(wb[:], sm[:, C_WB:C_WB + 1], base + 5 + (1 if own else 0), bias=my[:])
                    act.wait_ge(small_rd, base + 5 + (1 if own else 0))
                if dwc:
                    finish(*dwc, 0)
                if j == 1 and prev:
                    read(vy[:], sm[:, C_YV:C_YV + 1], base + 2)
                if j == 10 and nxt:
                    x_norm_read(1, base + k + (4 if prev else 3))
                if own and j < CHUNKS - 1:
                    sides(b, j + 1)
                elif nxt:
                    sides(b + 1, 0)
                if dwc:
                    finish(*dwc, 1)
                if j == 1 and prev:
                    read(hid[:], sm[0:HID, C_HID:C_HID + 1], base + 3, ACT.Relu, bias=b1c[:])
                if j == 1 and own:
                    read(db[:], dc[:, 0, C_DB:C_DB + 1], base + (4 if prev else 1), bias=bd[:])
                if j == CHUNKS - 1 and nxt:
                    off_bias(base + k + (5 if prev else 4))

            all_steps(act, step)

        @block.vector
        def _(dve):
            def evacuate(b, j, h):
                n, s = cid(b, j), j % CS
                dve.wait_ge(dcn_mm, 2 * n + h + 1)
                if h == 0:
                    dve.wait_ge(y_in[s], ring_total(b, j, CS, lambda i: 1))
                    if j == 0:
                        dve.wait_ge(small_rd, bias_read(b))
                        if not (isinstance(b, int) and b == 0):
                            dve.wait_ge(y_tot, b)
                y = yc[s][:, HALF * h:HALF * h + HALF, :].rearrange("p k w -> p (k w)")
                nc.vector.scalar_tensor_tensor(out=y, in0=dc[:, h, 0:NH], scalar=db[:], in1=y,
                                               op0=ALU.add, op1=ALU.add,
                                               accum_out=ys1[:, 2 * j + h:2 * j + h + 1])\
                    .then_inc(y_done, 1)

            def sample(b, j, early):
                n, s, v = cid(b, j), j % 2, xv[j % XS]
                at = n * LERPS
                q = nb[s]
                own = v[:, MID, :, 1:W + 1]
                dve.wait_ge(sided, n + 1)
                wait_apart(dve, prepped, 4 * n + 1)
                m3 = mu[s][:].bitcast(U16).unsqueeze(1).to_broadcast([P, 3, NB, W])
                nc.vector.copy_predicated(q[:, :, :, 1:W - 1], m3[:, :, :, 1:W - 1],
                                          v[:, :, :, 3:W + 1]).then_inc(lerp, 1)
                dve.wait_ge(lerp, at + 1)
                nc.vector.tensor_tensor(q[:, MID], q[:, MID], own, ALU.subtract).then_inc(lerp, 1)
                dve.wait_ge(lerp, at + 2)
                dve.wait_ge(prepped, 4 * n + 2)
                nc.vector.tensor_tensor(q[:, MID], q[:, MID], du[s][:], ALU.mult).then_inc(lerp, 1)
                dve.wait_ge(lerp, at + 3)
                nc.vector.tensor_tensor(q[:, MID], q[:, MID], own, ALU.add).then_inc(lerp, 1)
                for d in early:
                    evacuate(*d, 0)
                m1 = mv[s][:].bitcast(U16)
                wait_apart(dve, prepped, 4 * n + 3)
                if j in (0, CHUNKS - 1):
                    wait_apart(dve, mirror, 2 * b + 1 + (j > 0))
                nc.vector.copy_predicated(v[:, ABOVE, :, 1:W + 1], m1, v[:, BELOW, :, 1:W + 1])
                nc.vector.copy_predicated(q[:, ABOVE], m1, q[:, BELOW]).then_inc(lerp, 1)
                chosen = v[:, ABOVE, :, 1:W + 1]
                dve.wait_ge(lerp, at + 5)
                nc.vector.tensor_tensor(q[:, ABOVE], q[:, ABOVE], chosen, ALU.subtract).then_inc(lerp, 1)
                for d in early:
                    evacuate(*d, 1)
                dve.wait_ge(lerp, at + 6)
                nc.vector.tensor_tensor(q[:, ABOVE], q[:, ABOVE], du[s][:], ALU.mult).then_inc(lerp, 1)
                dve.wait_ge(lerp, at + 7)
                nc.vector.tensor_tensor(q[:, ABOVE], q[:, ABOVE], chosen, ALU.add).then_inc(x_free, 1)
                dve.wait_ge(x_free, n + 1)
                nc.vector.tensor_tensor(q[:, ABOVE], q[:, ABOVE], q[:, MID], ALU.subtract).then_inc(lerp, 1)
                dve.wait_ge(lerp, at + 8)
                dve.wait_ge(prepped, 4 * n + 4)
                nc.vector.tensor_tensor(q[:, ABOVE], q[:, ABOVE], dv[s][:], ALU.mult).then_inc(lerp, 1)
                if j == 0:
                    nc.vector.tensor_copy(mxs[:], mx[:]).then_inc(mxs_ok, 1)
                    dve.wait_ge(mxs_ok, b + 1)
                pj = j - 2
                pb = b if pj >= 0 else b - 1
                if not (isinstance(pb, int) and pb < 0):
                    dve.wait_ge(s_sh[pj % CHUNKS % SS], ring_total(pb, pj % CHUNKS, SS, s_dmas))
                nc.vector.tensor_scalar(sc[s][:, :, 0:WP:WP - 1], zero[:, 0:2 * NB].rearrange(
                    "p (k e) -> p k e", e=2), mxs[:], None, ALU.add)
                if j == 0:
                    wait(dve, dcn_mm, 2 * (n - 2))
                    nc.vector.tensor_scalar(sa[0:C, 0, :], zero[0:C, 0:WP], mxs[0:C], None, ALU.add)
                if j == CHUNKS - 1:
                    dve.wait_ge(dcn_mm, 2 * (n - 2))
                    nc.vector.tensor_scalar(sw[P - C:P, SS * NB - 1, :], zero[P - C:P, 0:WP],
                                            mxs[P - C:P], None, ALU.add)
                dve.wait_ge(lerp, at + 9)
                nc.vector.tensor_tensor(sc[s][:, :, 1:W + 1], q[:, ABOVE], q[:, MID], ALU.add)\
                    .then_inc(sampled, 1)

            dve.wait_ge(cleared, 2)
            dve.wait_ge(piv, 1)
            for i in range(STILES):
                dve.wait_ge(first_in[i], 16)
                wait(dve, first_sum, i)
                nc.vector.scalar_tensor_tensor(
                    out=st[0][:], in0=first_tile(ya, i), scalar=npiv[:],
                    in1=zero[:, 0:1].to_broadcast([P, SW]), op0=ALU.add, op1=ALU.add,
                    accum_out=xs1[:, i:i + 1]).then_inc(first_sum, 1)

            def step(b, j, own, nxt, prev, prev2):
                dcs = dcn_at(b, j, own, prev)
                early = dcs[:1] if own and j == 0 else []
                if own:
                    sample(b, j, early)
                for d in dcs[len(early):]:
                    for h in range(2):
                        evacuate(*d, h)

            all_steps(dve, step)

        @block.gpsimd
        def _(pool):
            ts, tt = nc.gpsimd.tensor_scalar, nc.gpsimd.tensor_tensor

            def pivot(b):
                if isinstance(b, int) and b == 0:
                    pool.wait_ge(first_in[0], 16)
                    ts(npiv[:], ya[:, 0, 0:1], -1.0, None, ALU.mult).then_inc(piv, 1)
                    return
                wait_apart(pool, st_in[0], (b - 1) * (16 * STILES // 2) + 16)
                ts(npiv[:], st[0][:, 0:1], -1.0, None, ALU.mult).then_inc(piv, 1)

            def x_norm(b, base):
                at = b * X_STEPS
                wait_apart(pool, x_tot, b + 1)
                tt(xn[:, M_LOC], xn[:, M_REL], npiv[:], ALU.subtract).then_inc(x_step, 1)
                tt(xn[:, M_SQ], xn[:, M_REL], xn[:, M_REL], ALU.mult).then_inc(x_step, 1)
                wait_apart(pool, x_step, at + 2)
                tt(xn[:, V_LOC], xn[:, V_SQ], xn[:, M_SQ], ALU.subtract).then_inc(x_step, 1)
                wait_apart(pool, small_rd, base + 1)
                ts(nmx[:], mx[:], -1.0, None, ALU.mult).then_inc(x_step, 1)
                wait_apart(pool, x_step, at + 4)
                tt(xn[:, DEV], xn[:, M_LOC], nmx[:], ALU.add).then_inc(x_step, 1)
                wait_apart(pool, x_step, at + 5)
                tt(xn[:, DEV_SQ], xn[:, DEV], xn[:, DEV], ALU.mult).then_inc(x_step, 1)
                wait_apart(pool, x_step, at + 6)
                tt(xn[:, V_ALL], xn[:, DEV_SQ], xn[:, V_LOC], ALU.add).then_inc(x_step, 1)
                wait_apart(pool, small_rd, base + 2)
                ts(xn[:, V_EPS], vx[:], EPS, None, ALU.add).then_inc(x_step, 1)
                wait_apart(pool, x_step, at + 8)
                tt(rx[:], xn[:, V_EPS], half[:], ALU.pow).then_inc(x_step, 1)
                wait_apart(pool, x_step, at + 9)

            def offset_weights(b):
                wait_apart(pool, off_mm, 2 * cid(b, 0))
                ts(wos[:], wo[:], rx[:], None, ALU.mult).then_inc(wo_ok, 1)

            def deform_weights(b):
                wait_apart(pool, dcn_mm, 2 * cid(b, 0))
                ts(wds[:], wd[:], rx[:], None, ALU.mult).then_inc(wd_ok, 1)

            def set_pads(b, j):
                n, v = cid(b, j), xv[j % XS]
                wait_apart(pool, off_mm, 2 * (n - XS + 1))
                if j == 0:
                    nc.gpsimd.tensor_copy(mxp[:], mx[:]).then_inc(mxp_ok, 1)
                    wait_apart(pool, mxp_ok, b + 1)
                if j in (0, CHUNKS - 1):
                    wait_apart(pool, x_free, n - XS + 1)
                    q, view, k = (slice(0, C), ABOVE, 0) if j == 0 else (slice(P - C, P), BELOW, NB - 1)
                    ts(v[q, view, k, 1:W + 1], zero[q, 0:W], mxp[q], None, ALU.add).then_inc(x_row, 1)
                    wait_apart(pool, x_row, 2 * b + (1 if j == 0 else 2))
                if j == CHUNKS - 1:
                    pool.sem_inc(pads, 1)
                    return
                for view in (ABOVE, BELOW):
                    last = ts(v[:, view, :, 0:WP:WP - 1],
                              zero[:, 0:2 * NB].rearrange("p (k e) -> p k e", e=2), mxp[:], None, ALU.add)
                last.then_inc(pads, 1)

            def y_norm(b, base, tap_count):
                at = b * Y_STEPS
                wait_apart(pool, y_tot, b + 1)
                tt(yn[:, M_REL], yn[:, M_LOC], nmy[:], ALU.add).then_inc(y_step, 1)
                wait_apart(pool, y_step, at + 1)
                tt(yn[:, M_SQ], yn[:, M_REL], yn[:, M_REL], ALU.mult).then_inc(y_step, 1)
                wait_apart(pool, y_step, at + 2)
                tt(yn[:, V_LOC], yn[:, V_SQ], yn[:, M_SQ], ALU.subtract).then_inc(y_step, 1)
                wait_apart(pool, small_rd, base + 1)
                ts(my_neg[:], my[:], -1.0, None, ALU.mult).then_inc(y_step, 1)
                wait_apart(pool, y_step, at + 4)
                tt(yn[:, DEV], yn[:, M_LOC], my_neg[:], ALU.add).then_inc(y_step, 1)
                wait_apart(pool, y_step, at + 5)
                tt(yn[:, DEV_SQ], yn[:, DEV], yn[:, DEV], ALU.mult).then_inc(y_step, 1)
                wait_apart(pool, y_step, at + 6)
                tt(yn[:, V_ALL], yn[:, DEV_SQ], yn[:, V_LOC], ALU.add).then_inc(y_step, 1)
                wait_apart(pool, small_rd, base + 2)
                ts(yn[:, V_EPS], vy[:], EPS, None, ALU.add).then_inc(y_step, 1)
                wait_apart(pool, y_step, at + 8)
                tt(ry[:], yn[:, V_EPS], half[:], ALU.pow).then_inc(y_step, 1)
                wait_apart(pool, y_step, at + 9)
                tt(yn[:, D_STD], yn[:, DEV], ry[:], ALU.mult).then_inc(y_step, 1)
                wait_apart(pool, y_step, at + 10)
                ts(pooled[:], yn[:, D_STD], 1.0 / G, None, ALU.mult).then_inc(y_step, 1)
                wait_apart(pool, dw_mm, 2 * cid(b, 0))
                edges = zero[:, 0:2 * BLOCKS].rearrange("p (k e) -> p k e", e=2)
                ts(ya[:, :, 0:WP:WP - 1], edges, my[:], None, ALU.add)
                ts(yb[:, :, 0:WP:WP - 1], edges, my[:], None, ALU.add).then_inc(y_row, 1)
                wait_apart(pool, y_row, 3 * b + 1)
                ts(ya[0:C, 0, 1:W + 1], zero[0:C, 0:W], my[0:C], None, ALU.add).then_inc(y_row, 1)
                wait_apart(pool, y_row, 3 * b + 2)
                q = slice(P - C, P)
                ts(yb[q, BLOCKS - 1, 1:W + 1], zero[q, 0:W], my[q], None, ALU.add).then_inc(y_row, 1)
                wait_apart(pool, y_row, 3 * b + 3)
                wait_apart(pool, small_rd, tap_count)
                tt(tap[:], tapr[:], b2r[:], ALU.add).then_inc(y_step, 1)
                wait_apart(pool, y_step, at + 12)
                ts(tap[:], tap[:], ry[:], None, ALU.mult).then_inc(y_step, 1)
                wait_apart(pool, y_step, at + 13)
                tt(tap[:], tap[:], kc[:, K_CEN], ALU.add).then_inc(y_step, 1)
                wait_apart(pool, y_step, at + 14)
                tt(wy[:].rearrange("p t (o c) -> p o t c", o=2),
                   kc[:, K_EYE].unsqueeze(1).unsqueeze(1).to_broadcast([P, 2, 3, C]),
                   tap[:].rearrange("p (o t) -> p o t", o=2).unsqueeze(3).to_broadcast([P, 2, 3, C]),
                   ALU.mult).then_inc(wy_ok, 1)

            nc.gpsimd.memset(zero[:], 0.0).then_inc(cleared, 1)
            nc.gpsimd.memset(half[:], -0.5).then_inc(cleared, 1)
            pool.wait_ge(cleared, 2)
            pivot(0)
            pool.wait_ge(loaded, LOADED)
            x_norm(0, 0)
            offset_weights(0)
            set_pads(0, 0)

            def step(b, j, own, nxt, prev, prev2):
                base = small_base(b)
                if j == 0:
                    if nxt:
                        pivot(b + 1)
                    if own:
                        set_pads(b, 1)
                        set_pads(b, 2)
                        deform_weights(b)
                if j == 1 and prev:
                    y_norm(b - 1, base, base + 4 + own)
                if j == 9 and nxt:
                    x_norm(b + 1, base + (6 if prev else 1))
                if j == 10 and own:
                    set_pads(b, CHUNKS - 1)
                if j == 11 and nxt:
                    set_pads(b + 1, 0)
                    offset_weights(b + 1)

            all_steps(pool, step)


def kernel(x, L0_conv_w_off, L0_conv_b_off, L0_conv_w_dcn, L0_conv_b_dcn, L1_conv_w1, L1_conv_b1,
           L1_conv_w2, L1_conv_b2):
    import concourse.bacc as bacc
    from concourse.bass_utils import run_bass_kernel_spmd

    p = np.arange(P)
    consts = np.zeros((P, P + C + 6), np.float32)
    consts[:, K_AVG] = (p[:, None] % C // 2 == p[None, :] % C // 2) / (2.0 * G)
    consts[:, K_EYE] = p[:, None] % C == np.arange(C)[None, :]
    for o in range(2):
        consts[:, P + C + 3 * o + 1] = p // C - o == 1
    asc = np.ascontiguousarray

    def bands(taps):
        full = np.zeros((G, *taps.shape[1:-1], 2, C), taps.dtype)
        for g, o in BANDS:
            full[g, ..., o, :] = taps[g - o]
        return full.reshape(P, *taps.shape[2:-1], 2 * C)

    by_ky = asc(L1_conv_w2).reshape(HID, C, 3, 3).transpose(2, 0, 3, 1)
    b_by_ky = asc(L1_conv_b2).reshape(C, 3, 3).transpose(1, 0, 2)
    w2 = np.zeros((HID, 2, 3, G, C), by_ky.dtype)
    b2 = np.zeros((G, C, 2, 3), b_by_ky.dtype)
    for g, o in BANDS:
        w2[:, o, :, g] = by_ky[g - o]
        b2[g, :, o] = b_by_ky[g - o]
    w2, b2 = w2.reshape(HID, 6, P), b2.reshape(P, 6)
    arrays = {
        "x": asc(np.asarray(x).transpose(0, 2, 1, 3)),
        "planes": asc(x),
        "w_off": bands(asc(L0_conv_w_off).reshape(C, 2, C, 3, 3).transpose(3, 2, 1, 4, 0)),
        "b_off": asc(np.tile(asc(L0_conv_b_off).reshape(C, 2), (G, 1))),
        "w_dcn": bands(asc(L0_conv_w_dcn).transpose(2, 1, 3, 0)),
        "b_dcn": asc(np.tile(asc(L0_conv_b_dcn).reshape(C, 1), (G, 1))),
        "w1": asc(np.tile(asc(L1_conv_w1), (G, 1))),
        "b1": asc(L1_conv_b1).reshape(HID, 1),
        "w2": w2,
        "b2": b2,
        "consts": consts,
    }
    nc = bacc.Bacc("TRN2", target_bir_lowering=False, num_devices=1)
    maps = {f"in_{name}": a for name, a in arrays.items()}
    args = [nc.dram_tensor(name, a.shape, mybir.dt.from_np(a.dtype), kind="ExternalInput").ap()
            for name, a in maps.items()]
    out = nc.dram_tensor("out", (B, P, BLOCKS, W), F32, kind="ExternalOutput").ap()
    block_kernel(nc, *args, out)
    got = run_bass_kernel_spmd(nc, [maps], core_ids=[0]).results[0]["out"]
    return asc(np.asarray(got).reshape(B, G, C, BLOCKS, W).transpose(0, 2, 3, 1, 4)).reshape(B, C, H, W)
```
